# Optimizing a Trainium2 kernel written in Bass

```python
import numpy as np
import jax
import jax.numpy as jnp

def _softmax(x, axis=-1):
    return jax.nn.softmax(x, axis=axis)

def _gelu(x):
    return jax.nn.gelu(x, approximate=True)

def _silu(x):
    return jax.nn.silu(x)

def _sigmoid(x):
    return jax.nn.sigmoid(x)

def _layernorm(x, axis=-1, eps=1e-05):
    m = jnp.mean(x, axis=axis, keepdims=True)
    v = jnp.var(x, axis=axis, keepdims=True)
    return (x - m) / jnp.sqrt(v + eps)

def _scatter_add(tgt, idx, src, axis=0):
    return tgt.at[idx].add(src)

def _segment_sum(src, seg, n):
    return jax.ops.segment_sum(src, seg, n)
kernel_name = 'mk_flamingo_gated_d1_seqx_r8_21f7b5'

def setup_inputs(seed: int=0):
    np.random.seed(seed)
    _w = jnp.asarray

    def _rec_inputs():
        import jax
        import jax.numpy as jnp
        _rk = jax.random.key(seed)
        x = -0.0003929 + 0.9999 * jax.random.normal(jax.random.fold_in(_rk, 1), (64, 64, 256), jnp.float32)
        _lenS = 64 - jax.random.randint(jax.random.fold_in(_rk, 7), (64,), 0, max(1, 64 // 4) + 1, jnp.int32)
        _lenS2 = 64 - jax.random.randint(jax.random.fold_in(_rk, 8), (64,), 0, max(1, 64 // 4) + 1, jnp.int32)
        _ctx_2048P = jax.random.normal(jax.random.fold_in(_rk, 11), (64, 16, 256), jnp.float32)
        _ctx_2048c = jax.random.dirichlet(jax.random.fold_in(_rk, 511), 0.3 * jnp.ones((16,), jnp.float32), (64, 64))
        _ctx_2048t = jnp.einsum('bsk,bkd->bsd', _ctx_2048c, _ctx_2048P)
        _ctx_2048t = _ctx_2048t * jax.lax.rsqrt(jnp.mean(jnp.square(_ctx_2048t)) + 1e-12) * 0.953939
        ctx_2048 = -0.000514642 + 1.00011 * (_ctx_2048t + 0.3 * jax.random.normal(jax.random.fold_in(_rk, 611), (64, 64, 256), jnp.float32))
        _g = jax.random.normal(jax.random.fold_in(_rk, 9001), (2, 1), jnp.float32)
        _g = jnp.sign(_g) * jnp.maximum(jnp.abs(_g), 1.0) + (_g == 0) * 1.0
        g_xattn = _g[0]
        g_ffn = _g[1]
        return (x, ctx_2048, g_xattn, g_ffn)
    x, ctx_2048, g_xattn, g_ffn = _rec_inputs()

    def _L0_xattn_setup():
        import jax, jax.numpy as jnp
        import numpy as np
        DIM = 256
        NHEADS = 32
        HEAD_DIM = DIM // NHEADS
        EPS = 1e-06

        def _rmsnorm(t):
            return t * jax.lax.rsqrt(jnp.mean(t * t, axis=-1, keepdims=True) + EPS)
        key = jax.random.key(seed)
        kx, kc, kq, kk, kv = jax.random.split(key, 5)
        x = jax.random.normal(kx, (2, 512, DIM), dtype=jnp.float32)
        context = jax.random.normal(kc, (2, 64, DIM), dtype=jnp.float32)
        std = 0.02
        Wq = jax.random.normal(kq, (DIM, DIM), dtype=jnp.float32) * std
        Wk = jax.random.normal(kk, (DIM, DIM), dtype=jnp.float32) * std
        Wv = jax.random.normal(kv, (DIM, DIM), dtype=jnp.float32) * std
        return {'x': x, 'context': context, 'Wq': Wq, 'Wk': Wk, 'Wv': Wv}
    _L0_xattn_all = _L0_xattn_setup()
    _L0_xattn_in = {k: v for k, v in _L0_xattn_all.items() if k in ('Wq', 'Wk', 'Wv')}
    del _L0_xattn_all

    def _L0_ffn_setup():
        import jax, jax.numpy as jnp
        import numpy as np
        DIM_IN = 256
        DIM_HIDDEN = 1024
        key = jax.random.key(seed)
        k_x, k_g, k_u, k_d = jax.random.split(key, 4)
        s_in = 1.0 / np.sqrt(DIM_IN)
        s_hid = 1.0 / np.sqrt(DIM_HIDDEN)
        x = jax.random.normal(k_x, (4, 256, DIM_IN), dtype=jnp.float32)
        w_gate = jax.random.uniform(k_g, (DIM_HIDDEN, DIM_IN), jnp.float32, -s_in, s_in)
        w_up = jax.random.uniform(k_u, (DIM_HIDDEN, DIM_IN), jnp.float32, -s_in, s_in)
        w_down = jax.random.uniform(k_d, (DIM_IN, DIM_HIDDEN), jnp.float32, -s_hid, s_hid)
        return {'x': x, 'w_gate': w_gate, 'w_up': w_up, 'w_down': w_down}
    _L0_ffn_all = _L0_ffn_setup()
    _L0_ffn_in = {k: v for k, v in _L0_ffn_all.items() if k in ('w_gate', 'w_up', 'w_down')}
    del _L0_ffn_all
    return {'x': x, 'ctx_2048': ctx_2048, 'g_xattn': g_xattn, 'g_ffn': g_ffn, 'L0_xattn_Wq': _L0_xattn_in['Wq'], 'L0_xattn_Wk': _L0_xattn_in['Wk'], 'L0_xattn_Wv': _L0_xattn_in['Wv'], 'L0_ffn_w_gate': _L0_ffn_in['w_gate'], 'L0_ffn_w_up': _L0_ffn_in['w_up'], 'L0_ffn_w_down': _L0_ffn_in['w_down']}

def reference(x, ctx_2048, g_xattn, g_ffn, L0_xattn_Wq, L0_xattn_Wk, L0_xattn_Wv, L0_ffn_w_gate, L0_ffn_w_up, L0_ffn_w_down):
    import jax
    import jax.numpy as jnp

    def _L0_xattn_ref(x, context, Wq, Wk, Wv):
        import jax, jax.numpy as jnp
        import numpy as np
        DIM = 256
        NHEADS = 32
        HEAD_DIM = DIM // NHEADS
        EPS = 1e-06

        def _rmsnorm(t):
            return t * jax.lax.rsqrt(jnp.mean(t * t, axis=-1, keepdims=True) + EPS)
        b, n, _ = x.shape
        m = context.shape[1]
        q = x @ Wq.T
        k_raw = context @ Wk.T
        v_raw = context @ Wv.T
        q = q.reshape(b, n, NHEADS, HEAD_DIM).transpose(0, 2, 1, 3)
        kv = jnp.concatenate([k_raw, v_raw], axis=-1)
        kv = kv.reshape(b, m, NHEADS, HEAD_DIM, 2)
        k = kv[..., 0].transpose(0, 2, 1, 3)
        v = kv[..., 1].transpose(0, 2, 1, 3)
        q = _rmsnorm(q)
        k = _rmsnorm(k)
        scale = HEAD_DIM ** (-0.5)
        scores = jnp.einsum('bhnd,bhmd->bhnm', q, k) * scale
        attn = jax.nn.softmax(scores, axis=-1)
        out = jnp.einsum('bhnm,bhmd->bhnd', attn, v)
        return out.transpose(0, 2, 1, 3).reshape(b, n, NHEADS * HEAD_DIM)

    def _L0_ffn_ref(x, w_gate, w_up, w_down):
        import jax, jax.numpy as jnp
        import numpy as np
        DIM_IN = 256
        DIM_HIDDEN = 1024
        gate = jnp.einsum('bsd,hd->bsh', x, w_gate)
        up = jnp.einsum('bsd,hd->bsh', x, w_up)
        gated = jax.nn.silu(gate) * up
        return jnp.einsum('bsh,dh->bsd', gated, w_down)
    x = x + jnp.tanh(g_xattn[0]) * _L0_xattn_ref(_layernorm(x, axis=-1), ctx_2048, L0_xattn_Wq, L0_xattn_Wk, L0_xattn_Wv)
    x = x + jnp.tanh(g_ffn[0]) * _L0_ffn_ref(_layernorm(x, axis=-1), L0_ffn_w_gate, L0_ffn_w_up, L0_ffn_w_down)
    return x

_drawn_inputs = setup_inputs


def setup_inputs(seed=0):
    import zlib

    import numpy as np

    out = dict(_drawn_inputs(seed))
    spreads = {}
    factors = {}
    for name, (base, spread) in spreads.items():
        noise = np.random.default_rng([zlib.crc32(name.encode()), seed]).standard_normal(out[name].shape)
        drawn = base * np.exp(spread * noise) if base else spread * noise
        out[name] = jnp.asarray(drawn.astype(out[name].dtype))
    for name, factor in factors.items():
        out[name] = (out[name] * factor).astype(out[name].dtype)
    return out
```

```python
import concourse.bass as bass
from concourse import mybir
from contextlib import ExitStack

F32 = mybir.dt.float32
F32R = mybir.dt.float32r
F16 = mybir.dt.float16
BF16 = mybir.dt.bfloat16
ALU = mybir.AluOpType
ACT = mybir.ActivationFunctionType
AX = mybir.AxisListType

BATCH, SEQ, DIM = 64, 64, 256
HEADS, HD = 32, 8
HIDDEN = 1024
P = 128
PAIRS = BATCH * SEQ // P
GROUP = 4
GROUPS = PAIRS // GROUP
KD = DIM // P
CH = HIDDEN // P
RND = 4
TPR = HEADS // 2 // RND
GRP_T = 8
VW = 3 * HD + 1
LN_EPS, RMS_EPS = 1e-5, 1e-6
SCALE = float(HD) ** -0.5

FFN_PIECES = [
    [("D", 0, 0), ("D", 0, 1), ("D", 1, 0), ("D", 1, 1), ("D", 2, 0), ("D", 2, 1)],
    [("D", 3, 0), ("D", 3, 1), ("G", 0), ("U", 0), ("G", 1), ("U", 1)],
    [("G", 2), ("U", 2), ("G", 3), ("U", 3), ("G", 4), ("U", 4)],
    [("G", 5), ("U", 5), ("G", 6), ("U", 6), ("G", 7), ("U", 7)],
]


class Slot:

    def __init__(self, turn, half, q):
        self.turn, self.half, self.q = turn, half, q
        self.grp = turn * 2 + half
        self.looped = not isinstance(turn, int)

    def count(self, per_pair, back, extra=0):
        return self.grp * (GROUP * per_pair) + (per_pair * (self.q - back) + extra)

    def group_count(self, per_group, back, extra=0):
        return self.grp * per_group + (extra - per_group * back)

    def has_pair(self, back):
        return self.looped or 0 <= GROUP * self.grp + self.q - back < PAIRS

    def buf(self, back, ring):
        return (GROUP * self.half + self.q - back) % ring

    def pieces(self):
        out = []
        for piece in FFN_PIECES[self.q]:
            back = 2 if piece[0] == "D" else 1
            ok = self.looped or 0 <= self.grp - back < GROUPS
            out.append(piece if ok else None)
        return out


def slots(eng, emit):
    two_groups = [(half, q) for half in range(2) for q in range(GROUP)]
    for half, q in two_groups:
        emit(Slot(0, half, q))
    with eng.Fori(1, GROUPS // 2) as turn:
        for half, q in two_groups:
            emit(Slot(turn, half, q))
    for half, q in two_groups[:GROUP + 2]:
        emit(Slot(GROUPS // 2, half, q))


def wait(eng, sem, value):
    if not isinstance(value, int) or value > 0:
        eng.wait_ge(sem, value)


def flamingo_block(nc, x, ctx_in, g_attn, g_ffn, w_qkv, w_up, w_down, out):
    x_t = x.rearrange("(i t b) s d -> i t (b s) d", b=P // SEQ, t=2 * GROUP)
    c_t = ctx_in.rearrange("(i t b) s d -> i t (b s) d", b=P // SEQ, t=2 * GROUP)
    out_g = out.rearrange("(i g t b) s d -> i g (b s) t d", b=P // SEQ, t=GROUP, g=2)
    wqkv_d = w_qkv.rearrange("(k p) n -> p k n", p=P)
    wup_d = w_up.rearrange("(k p) n -> p k n", p=P)
    wdn_d = w_down.rearrange("(k p) n -> p k n", p=P)

    stack = ExitStack()
    with stack:
        def sb(name, shape, dt=F32):
            return stack.enter_context(nc.sbuf_tensor(name, shape, dt))

        def sem(name):
            return stack.enter_context(nc.semaphore(name))

        wqkv_hi, wqkv_lo = (sb(f"wqkv_{n}", [P, KD, 3 * DIM], F32R) for n in ("hi", "lo"))
        wup_hi, wup_lo = (sb(f"wup_{n}", [P, KD, 2 * HIDDEN], F32R) for n in ("hi", "lo"))
        wdn_hi, wdn_lo = (sb(f"wdn_{n}", [P, CH, DIM], F32R) for n in ("hi", "lo"))
        stage = sb("stage", [P, 2, 1024])
        ident32 = sb("ident32", [P, P])
        ident16 = sb("ident16", [P, P], F16)
        neg_half = sb("neg_half", [P, 64])
        eps = sb("eps", [P, 2])
        gates = sb("gates", [P, 2])
        tgates = sb("tgates", [P, 2])
        ffn_gate = sb("ffn_gate", [P, 1])

        xbuf = sb("xbuf", [P, 4, DIM])
        cbuf = sb("cbuf", [P, 4, DIM])
        st1, mv1, ve1, rstd1 = sb("st1", [P, 6]), sb("mv1", [P, 2]), sb("ve1", [P, 1]), sb("rstd1", [P, 1])
        st2, mv2, ve2, rstd2 = sb("st2", [P, 6]), sb("mv2", [P, 2]), sb("ve2", [P, 1]), sb("rstd2", [P, 1])
        spare = sb("spare", [P, 2])
        xn = sb("xn", [P, 2, DIM])
        tT_hi, tT_lo = (sb(f"tT_{n}", [P, 2 * KD, P], F32R) for n in ("hi", "lo"))
        sq = sb("sq", [P, 2 * DIM])
        ss, ms, rqk = sb("ss", [P, 2 * HEADS]), sb("ms", [P, 2 * HEADS]), sb("rqk", [P, 2 * HEADS])
        qk32 = sb("qk32", [P, 2 * DIM])
        q4 = sb("q4", [P, HEADS, 4, HD], F16)
        k4 = sb("k4", [P, HEADS, 4, HD], F16)
        qT = sb("qT", [P, GRP_T, 2, SEQ], F16)
        kT = sb("kT", [P, GRP_T, 2, 2, 2, SEQ], F16)
        vrem = sb("vrem", [P, DIM])
        vn = sb("vn", [P, HEADS, 3, HD], BF16)
        vp_flat = sb("vp", [P, 4 * HEADS * VW], BF16)
        vp = vp_flat[:, :].rearrange("p (u t b a c) -> p u t b a c", u=2, b=2, a=2, c=VW)
        p32 = sb("p32", [P, RND, 512])
        p_hi = sb("p_hi", [P, RND, 512], F16)
        p_lo = sb("p_lo", [P, RND, 512], F16)
        oa = sb("oa", [P, HEADS, VW])
        asum = sb("asum", [P, DIM])
        rinv = sb("rinv", [P, HEADS])
        xr = sb("xr", [P, 8, DIM])
        yn = sb("yn", [P, 2, DIM])
        yT_hi, yT_lo = (sb(f"yT_{n}", [P, 2, KD, 512], F32R) for n in ("hi", "lo"))
        hb = sb("hb", [P, 2, 512])
        h_hi, h_lo = (sb(f"h_{n}", [P, CH, 512], F32R) for n in ("hi", "lo"))
        obuf = sb("obuf", [P, GROUP, DIM])

        bank = [stack.enter_context(nc.psum_tensor(f"bank{i}", [P, 512], F32)) for i in range(8)]
        ffn_ps = bank[0:2]
        tr_ps, qk_ps, v_ps, o_ps = bank[2], bank[3], bank[4], bank[5]
        s_ps = bank[6:8]
        qT_ps = tr_ps[:, :].bitcast(F16)
        kT_ps = qk_ps[:, :].bitcast(F16)
        y_ps = v_ps

        names = """x_in0 x_in1 x_in2 x_in3 c_in0 c_in1 c_in2 c_in3 w_in0 w_in1 gate_in out_stored
            zeroed ident_made const_made w_hi w_lo tanh_g gate_half
            bn1 mv1_done ve1_done rstd1_done xn_done tr_done tT_hi_done tT_lo_done qk_done v_done
            sq_done ss_done ms_done rqk_done norm_done hi_qk lo_qk qT_tr kT_tr qT_done kT_done
            v1_done vrem_done v2_done v3_done vp_done s_done p32_done p_hi_done p_lo_done pv_done
            o_done asum_done rinv_done attn_done x1_done bn2 mv2_done ve2_done rstd2_done yn_done
            y_tr yT_hi_done yT_lo_done up_done tanh_done gt_done h_done h_hi_done h_lo_done
            down_done out_ready""".split()
        S = {n: sem(n) for n in names}
        x_in = [S[f"x_in{i}"] for i in range(4)]
        c_in = [S[f"c_in{i}"] for i in range(4)]
        w_in = [S[f"w_in{i}"] for i in range(2)]

        pieces = [(wqkv_d[:, k, :], wqkv_hi[:, k, :], wqkv_lo[:, k, :]) for k in range(KD)]
        for k in range(KD):
            for u in range(2):
                c = slice(u * HIDDEN, (u + 1) * HIDDEN)
                pieces.append((wup_d[:, k, c], wup_hi[:, k, c], wup_lo[:, k, c]))
        for u in range(2):
            c = slice(4 * u, 4 * u + 4)
            flat = "p k n -> p (k n)"
            pieces.append((wdn_d[:, c, :], wdn_hi[:, c, :].rearrange(flat), wdn_lo[:, c, :].rearrange(flat)))
        QKV_PIECES, UP_PIECES = KD, 3 * KD

        def staged(i):
            return stage[:, i % 2, 0:pieces[i][1].shape[1]]

        def split_in_slot(s):
            if s.looped or s.grp > 0 or s.q > 2:
                return []
            return [QKV_PIECES + 2 * s.q, QKV_PIECES + 2 * s.q + 1]

        block = stack.enter_context(nc.Block())

        @block.sync
        def _(sp):
            def load_weights(i):
                if i >= 2:
                    sp.wait_ge(S["w_lo"], i - 1)
                dst = staged(i)
                if i >= UP_PIECES:
                    dst = dst.rearrange("p (k n) -> p k n", n=DIM)
                sp.dma_start(dst, pieces[i][0]).then_inc(w_in[i % 2], 16)

            def load_pair(s):
                pair = GROUP * s.half + s.q
                wait(sp, S["x1_done"], s.count(1, 3))
                sp.dma_start(xbuf[:, s.q, :], x_t[s.turn, pair, :, :]).then_inc(x_in[s.q], 16)
                sp.dma_start(cbuf[:, s.q, :], c_t[s.turn, pair, :, :]).then_inc(c_in[s.q], 16)

            load_pair(Slot(0, 0, 0))
            load_weights(0)
            load_weights(1)
            for q in range(1, GROUP):
                load_pair(Slot(0, 0, q))
            for col, g in enumerate((g_attn, g_ffn)):
                sp.dma_start(gates[:, col:col + 1], g.partition_broadcast(P)).then_inc(S["gate_in"], 16)
            for i in range(2, len(pieces)):
                load_weights(i)
            for q in range(GROUP):
                load_pair(Slot(0, 1, q))
            with sp.Fori(1, GROUPS // 2) as turn:
                for half in range(2):
                    for q in range(GROUP):
                        load_pair(Slot(turn, half, q))

        @block.tensor
        def _(pe):
            mm = nc.tensor.matmul

            def product(o, left, right, first, last):
                (lh, ll), (rh, rl) = left, right
                mm(o, lh, rh, start=first, stop=False)
                mm(o, lh, rl, start=False, stop=False)
                return mm(o, ll, rh, start=False, stop=last)

            def transposes(s):
                pe.wait_ge(c_in[s.q], s.group_count(16, -1))
                wait(pe, S["qT_done"], s.count(1, 0))
                pe.wait_ge(S["xn_done"], s.count(1, -1))
                for k in range(KD):
                    nc.tensor.transpose(tr_ps[:, k * P:(k + 1) * P], xn[:, s.buf(0, 2), k * P:(k + 1) * P],
                                        ident32[:, :])
                for k in range(KD):
                    last = nc.tensor.transpose(tr_ps[:, (KD + k) * P:(KD + k + 1) * P],
                                               cbuf[:, s.q, k * P:(k + 1) * P], ident32[:, :])
                last.then_inc(S["tr_done"], 1)

            def project(s):
                pe.wait_ge(S["tT_hi_done"], s.count(1, -1))
                pe.wait_ge(S["tT_lo_done"], s.count(1, -1))
                wait(pe, S["yT_lo_done"], s.count(1, 2))

                def one(o, part, col):
                    for k in range(KD):
                        last = product(o, (tT_hi[:, KD * part + k, :], tT_lo[:, KD * part + k, :]),
                                       (wqkv_hi[:, k, col:col + DIM], wqkv_lo[:, k, col:col + DIM]),
                                       k == 0, k == KD - 1)
                    return last

                one(v_ps[:, 0:DIM], 1, 2 * DIM).then_inc(S["v_done"], 1)
                wait(pe, S["kT_done"], s.count(1, 0))
                one(qk_ps[:, 0:DIM], 0, 0)
                one(qk_ps[:, DIM:2 * DIM], 1, DIM).then_inc(S["qk_done"], 1)

            def qk_transposes(s):
                pe.wait_ge(S["hi_qk"], s.count(2, -1))
                pe.wait_ge(S["lo_qk"], s.count(1, -1))
                q_rows = q4[:, :, :, :].rearrange("p (g h) c d -> p g (h c d)", g=GRP_T)
                k_rows = k4[:, :, :, :].rearrange("p (g h) c d -> p g (h c d)", g=GRP_T)
                for rows, ps, done in ((q_rows, qT_ps, "qT_tr"), (k_rows, kT_ps, "kT_tr")):
                    for g in range(GRP_T):
                        last = nc.tensor.transpose(ps[:, g * P:(g + 1) * P], rows[:, g, :], ident16[:, :])
                    last.then_inc(S[done], 1)

            def scores(s, r):
                if r == 0:
                    pe.wait_ge(S["qT_done"], s.count(1, 0))
                    pe.wait_ge(S["kT_done"], s.count(1, 0))
                wait(pe, S["p_hi_done"], s.count(RND, 1, r - 1))
                o = s_ps[r % 2][:, :].rearrange("p (t b n) -> p t b n", t=TPR, b=2)
                for tt in range(TPR):
                    g, pair = divmod(TPR * r + tt, 2)
                    for b in range(2):
                        last = mm(o[:, tt, b, :], kT[:, g, b, pair, :, :].rearrange("p a m -> p (a m)"),
                                  qT[:, g, b, :], start=True, stop=True)
                last.then_inc(S["s_done"], 1)

            def attend(s, r):
                if r == 0:
                    pe.wait_ge(S["vp_done"], s.count(1, 0))
                pe.wait_ge(S["p_lo_done"], s.count(RND, 1, r + 1))
                wait(pe, S["o_done"], s.count(RND, 1, r))
                o = o_ps[:, 0:TPR * 4 * VW].rearrange("p (t c) -> p t c", t=TPR)
                for tt in range(TPR):
                    values = vp[:, s.buf(1, 2), TPR * r + tt, :, :, :].rearrange("p b a c -> p (b a) c")
                    cols = slice(tt * P, (tt + 1) * P)
                    mm(o[:, tt, :], p_hi[:, r, cols], values.rearrange("p a c -> p (a c)"), start=True, stop=False)
                    last = mm(o[:, tt, :].rearrange("p (a c) -> p a c", c=VW)[:, :, HD:VW],
                              p_lo[:, r, cols], values[:, :, HD:VW], start=False, stop=True)
                last.then_inc(S["pv_done"], 1)

            def y_transposes(s):
                pe.wait_ge(S["yn_done"], s.count(1, 1))
                if s.has_pair(0):
                    pe.wait_ge(S["vrem_done"], s.count(1, -1))
                for k in range(KD):
                    last = nc.tensor.transpose(y_ps[:, k * P:(k + 1) * P], yn[:, s.buf(2, 2), k * P:(k + 1) * P],
                                               ident32[:, :])
                last.then_inc(S["y_tr"], 1)

            def ffn_piece(s, piece):
                if piece is None:
                    return
                if piece[0] == "D":
                    _, j, part = piece
                    if (j, part) == (0, 0):
                        pe.wait_ge(S["h_hi_done"], s.group_count(CH, 1))
                        pe.wait_ge(S["h_lo_done"], s.group_count(CH, 1))
                        if not s.looped:
                            pe.wait_ge(S["w_lo"], len(pieces))
                    if j >= 2 and part == 0:
                        pe.wait_ge(S["out_ready"], s.group_count(GROUP, 2, j - 1))
                    o = ffn_ps[j % 2][:, 0:DIM]
                    tok = slice(j * P, (j + 1) * P)
                    for c in range(CH // 2 * part, CH // 2 * (part + 1)):
                        last = product(o, (h_hi[:, c, tok], h_lo[:, c, tok]), (wdn_hi[:, c, :], wdn_lo[:, c, :]),
                                       c == 0, c == CH - 1)
                    if part:
                        last.then_inc(S["down_done"], 1)
                    return
                up, c = piece[0] == "U", piece[1]
                if c == 0:
                    if not up:
                        pe.wait_ge(S["yT_hi_done"], s.group_count(GROUP, 0))
                        pe.wait_ge(S["yT_lo_done"], s.group_count(GROUP, 0))
                        if not s.looped:
                            pe.wait_ge(S["w_lo"], UP_PIECES)
                    wait(pe, S["out_ready"], s.group_count(GROUP, 2, 4 if up else 3)
                         if s.looped or s.grp > 1 else 0)
                else:
                    pe.wait_ge(S["h_done" if up else "gt_done"], s.group_count(CH, 1, c))
                col = slice(up * HIDDEN + c * P, up * HIDDEN + (c + 1) * P)
                half = 1 - s.half
                for k in range(KD):
                    last = product(ffn_ps[up][:, :], (wup_hi[:, k, col], wup_lo[:, k, col]),
                                   (yT_hi[:, half, k, :], yT_lo[:, half, k, :]), k == 0, k == KD - 1)
                last.then_inc(S["up_done"], 1)

            pe.wait_ge(S["ident_made"], 2)
            pe.wait_ge(S["zeroed"], 3)

            def emit(s):
                X = s.pieces()
                ffn_piece(s, X[0])
                if s.has_pair(1):
                    scores(s, 0)
                    scores(s, 1)
                if s.has_pair(0):
                    transposes(s)
                ffn_piece(s, X[1])
                if s.has_pair(0):
                    if not s.looped and s.grp + s.q == 0:
                        pe.wait_ge(S["w_lo"], QKV_PIECES)
                    project(s)
                if s.has_pair(1):
                    scores(s, 2)
                    scores(s, 3)
                if s.has_pair(2):
                    y_transposes(s)
                ffn_piece(s, X[2])
                if s.has_pair(1):
                    attend(s, 0)
                ffn_piece(s, X[3])
                if s.has_pair(1):
                    attend(s, 1)
                ffn_piece(s, X[4])
                if s.has_pair(0):
                    qk_transposes(s)
                if s.has_pair(1):
                    attend(s, 2)
                ffn_piece(s, X[5])
                if s.has_pair(1):
                    attend(s, 3)

            slots(pe, emit)

        @block.scalar
        def _(act):
            def split_weights(i):
                act.wait_ge(w_in[i % 2], 16 * (i // 2 + 1))
                nc.scalar.activation(pieces[i][1], staged(i), ACT.Copy).then_inc(S["w_hi"], 1)

            def exps(s, r):
                act.wait_ge(S["s_done"], s.count(RND, 1, r + 1))
                nc.scalar.activation(p32[:, r, :], s_ps[r % 2][:, :], ACT.Exp, scale=SCALE).then_inc(S["p32_done"], 1)
                nc.scalar.activation(p_hi[:, r, :], s_ps[r % 2][:, :], ACT.Exp, scale=SCALE).then_inc(S["p_hi_done"], 1)

            def t_hi(s):
                act.wait_ge(S["tr_done"], s.count(1, -1))
                nc.scalar.activation(tT_hi[:, :, :].rearrange("p k n -> p (k n)"), tr_ps[:, :],
                                     ACT.Copy).then_inc(S["tT_hi_done"], 1)

            def v_and_squares(s):
                act.wait_ge(S["v_done"], s.count(1, -1))
                wait(act, S["vp_done"], s.count(1, 0))
                nc.scalar.activation(vn[:, :, 1, :], v_ps[:, 0:DIM].rearrange("p (h d) -> p h d", d=HD),
                                     ACT.Copy).then_inc(S["v1_done"], 1)
                act.wait_ge(S["qk_done"], s.count(1, -1))
                nc.scalar.activation(sq[:, :], qk_ps[:, :], ACT.Square, scale=float(HD) ** -0.5).then_inc(S["sq_done"], 1)

            def v_second(s):
                act.wait_ge(S["vrem_done"], s.count(1, -1))
                nc.scalar.activation(vn[:, :, 2, :], vrem[:, :].rearrange("p (h d) -> p h d", d=HD),
                                     ACT.Copy).then_inc(S["v2_done"], 1)

            def y_hi(s):
                act.wait_ge(S["y_tr"], s.count(1, 1))
                j = (s.q - 2) % GROUP
                half = s.half if s.q >= 2 else 1 - s.half
                nc.scalar.activation(yT_hi[:, half, :, j * P:(j + 1) * P],
                                     y_ps[:, 0:DIM].rearrange("p (k n) -> p k n", k=KD),
                                     ACT.Copy).then_inc(S["yT_hi_done"], 1)

            def k_blocks(s):
                act.wait_ge(S["kT_tr"], s.count(1, -1))
                for j in range(4):
                    rows = slice(32 * j, 32 * j + 32)
                    last = nc.scalar.activation(kT[rows, :, :, j // 2, j % 2, :],
                                                kT_ps[rows, :].rearrange("p (g b m) -> p g b m", g=GRP_T, b=2),
                                                ACT.Copy)
                last.then_inc(S["kT_done"], 1)

            def take_o(s, r):
                act.wait_ge(S["pv_done"], s.count(RND, 1, r + 1))
                for b in range(2):
                    rows = slice(SEQ * b, SEQ * (b + 1))
                    o = o_ps[rows, 0:TPR * 4 * VW].rearrange("p (t b c) -> p t b c", t=TPR, b=2)
                    to = oa[rows, 2 * TPR * r:2 * TPR * (r + 1), :].rearrange("p (t a) c -> p t (a c)", a=2)
                    last = nc.scalar.activation(to, o[:, :, b, :], ACT.Copy)
                last.then_inc(S["o_done"], 1)

            def ffn_event(s, i):
                piece = s.pieces()[i]
                if piece is None or piece[0] == "D":
                    return
                c = piece[1]
                if piece[0] == "G":
                    act.wait_ge(S["up_done"], s.group_count(2 * CH, 1, 2 * c + 1))
                    wait(act, S["h_lo_done"], s.group_count(CH, 1, c - 1))
                    nc.scalar.activation(hb[:, c % 2, :], ffn_ps[0][:, :], ACT.Tanh,
                                         scale=0.5).then_inc(S["tanh_done"], 1)
                else:
                    act.wait_ge(S["h_done"], s.group_count(CH, 1, c + 1))
                    nc.scalar.activation(h_hi[:, c, :], hb[:, c % 2, :], ACT.Copy).then_inc(S["h_hi_done"], 1)

            def store_out(s):
                act.wait_ge(S["out_ready"], s.group_count(GROUP, 1))
                act.dma_start(out_g[s.turn - 1, s.half, :, :, :], obuf[:, :, :]).then_inc(S["out_stored"], 16)

            for i in range(QKV_PIECES):
                split_weights(i)
            act.wait_ge(S["gate_in"], 32)
            nc.scalar.activation(tgates[:, :], gates[:, :], ACT.Tanh).then_inc(S["tanh_g"], 1)

            def emit(s):
                down = s.looped or 2 <= s.grp
                ffn_event(s, 0)
                if s.has_pair(1):
                    exps(s, 0)
                if s.has_pair(0):
                    t_hi(s)
                if s.has_pair(1):
                    exps(s, 1)
                ffn_event(s, 1)
                if s.has_pair(0):
                    v_and_squares(s)
                if s.has_pair(1):
                    exps(s, 2)
                if s.has_pair(0):
                    v_second(s)
                if s.has_pair(1):
                    exps(s, 3)
                if s.has_pair(2):
                    y_hi(s)
                if down and s.q == 1:
                    store_out(s)
                ffn_event(s, 2)
                if s.has_pair(1):
                    take_o(s, 0)
                ffn_event(s, 3)
                if s.has_pair(1):
                    take_o(s, 1)
                ffn_event(s, 4)
                if s.has_pair(0):
                    k_blocks(s)
                if s.has_pair(1):
                    take_o(s, 2)
                if down and s.q == 3:
                    act.wait_ge(S["out_stored"], s.group_count(16, 1))
                if s.has_pair(1):
                    take_o(s, 3)
                ffn_event(s, 5)
                for i in split_in_slot(s):
                    split_weights(i)

            act.wait_ge(S["zeroed"], 1)
            slots(act, emit)
            act.wait_ge(S["out_stored"], 16 * GROUPS)

        @block.vector
        def _(dve):
            v = nc.vector
            v.memset(kT[:, :, :, :, :, :].rearrange("p g b i j m -> p (g b i j m)").bitcast(F32), 0.0).then_inc(S["zeroed"], 1)
            v.memset(neg_half[:, :], -0.5).then_inc(S["const_made"], 1)
            v.memset(vp_flat[:, :].bitcast(F32), 0.0).then_inc(S["zeroed"], 1)
            dve.wait_ge(S["zeroed"], 2)
            for a in range(2):
                last = v.memset(vp[SEQ * a:SEQ * (a + 1), :, :, :, a, 3 * HD:VW], 1.0)
            last.then_inc(S["zeroed"], 1)

            def split_weights(i):
                dve.wait_ge(S["w_hi"], i + 1)
                v.tensor_tensor(pieces[i][2], staged(i), pieces[i][1].bitcast(F32), ALU.subtract).then_inc(S["w_lo"], 1)

            def first_stats(s):
                dve.wait_ge(x_in[s.q], s.group_count(16, -1))
                v.bn_stats(st1[:, :], xbuf[:, s.q, :]).then_inc(S["bn1"], 1)
                dve.wait_ge(S["bn1"], s.count(1, -1))
                v.memset(spare[:, 0:1], 0.0)
                v.bn_aggr(mv1[:, :], st1[:, :]).then_inc(S["mv1_done"], 1)

            def first_norm(s):
                dve.wait_ge(S["rstd1_done"], s.count(1, -1))
                v.tensor_scalar(xn[:, s.buf(0, 2), :], xbuf[:, s.q, :], mv1[:, 0:1], rstd1[:, 0:1],
                                ALU.subtract, ALU.mult).then_inc(S["xn_done"], 1)

            def t_lo(s):
                dve.wait_ge(S["tT_hi_done"], s.count(1, -1))
                flat = "p k n -> p (k n)"
                v.tensor_tensor(tT_lo[:, :, :].rearrange(flat), tr_ps[:, :],
                                tT_hi[:, :, :].rearrange(flat).bitcast(F32), ALU.subtract).then_inc(S["tT_lo_done"], 1)

            def v_rest(s):
                dve.wait_ge(S["v1_done"], s.count(1, -1))
                v.tensor_tensor(vrem[:, :].rearrange("p (h d) -> p h d", d=HD),
                                v_ps[:, 0:DIM].rearrange("p (h d) -> p h d", d=HD), vn[:, :, 1, :],
                                ALU.subtract).then_inc(S["vrem_done"], 1)

            def sums_of_squares(s):
                dve.wait_ge(S["sq_done"], s.count(1, -1))
                v.tensor_reduce(ss[:, :], sq[:, :].rearrange("p (h d) -> p h d", d=HD), AX.X, ALU.add).then_inc(S["ss_done"], 1)

            def qk_norm(s):
                dve.wait_ge(S["rqk_done"], s.count(1, -1))
                v.tensor_tensor(qk32[:, :].rearrange("p (h d) -> p h d", d=HD),
                                qk_ps[:, :].rearrange("p (h d) -> p h d", d=HD),
                                rqk[:, :].unsqueeze(2).broadcast_to([P, 2 * HEADS, HD]), ALU.mult).then_inc(S["norm_done"], 1)

            def qk_lo(s):
                dve.wait_ge(S["hi_qk"], s.count(2, -1))
                qk = qk32[:, :].rearrange("p (w h d) -> p w h d", w=2, d=HD)
                for w, (rows, slots_) in enumerate(((q4, slice(2, 4)), (k4, slice(1, 4, 2)))):
                    hi = rows[:, :, 0, :]
                    last = v.tensor_tensor(rows[:, :, slots_, :], qk[:, w, :, :].unsqueeze(2).broadcast_to([P, HEADS, 2, HD]),
                                           hi.unsqueeze(2).broadcast_to([P, HEADS, 2, HD]), ALU.subtract)
                last.then_inc(S["lo_qk"], 1)

            def lay_out_values(s):
                dve.wait_ge(S["v3_done"], s.count(1, -1))
                for a in range(2):
                    for b in range(2):
                        src = vn[SEQ * b:SEQ * (b + 1), :, :, :].rearrange("p (t a) c d -> p t a (c d)", a=2)
                        last = v.tensor_copy(vp[SEQ * a:SEQ * (a + 1), s.buf(0, 2), :, b, a, 0:3 * HD], src[:, :, a, :])
                last.then_inc(S["vp_done"], 1)

            def p_rest(s, r):
                dve.wait_ge(S["p_hi_done"], s.count(RND, 1, r + 1))
                v.tensor_tensor(p_lo[:, r, :], p32[:, r, :], p_hi[:, r, :], ALU.subtract).then_inc(S["p_lo_done"], 1)

            def take_q(s):
                dve.wait_ge(S["qT_tr"], s.count(1, -1))
                v.tensor_copy(qT[:, :, :, :].rearrange("p g b n -> p (g b n)"), qT_ps[:, :]).then_inc(S["qT_done"], 1)

            def attention_sums(s):
                dve.wait_ge(S["o_done"], s.count(RND, 1))
                parts = oa[:, :, 0:3 * HD].rearrange("p h (c d) -> p h d c", d=HD)
                v.tensor_reduce(asum[:, :].rearrange("p (h d) -> p h d", d=HD), parts, AX.X, ALU.add).then_inc(S["asum_done"], 1)
                v.reciprocal(rinv[:, :], oa[:, :, 3 * HD]).then_inc(S["rinv_done"], 1)

            def residual(s):
                dve.wait_ge(S["rinv_done"], s.count(1, 1))
                a3 = asum[:, :].rearrange("p (h d) -> p h d", d=HD)
                v.tensor_tensor(a3, a3, rinv[:, :].unsqueeze(2).broadcast_to([P, HEADS, HD]), ALU.mult).then_inc(S["attn_done"], 1)
                dve.wait_ge(S["attn_done"], s.count(1, 1))
                x1 = xr[:, s.buf(2, 8), :]
                v.scalar_tensor_tensor(out=x1, in0=asum[:, :], scalar=tgates[:, 0:1], in1=xbuf[:, s.buf(2, 4), :],
                                       op0=ALU.mult, op1=ALU.add).then_inc(S["x1_done"], 1)
                dve.wait_ge(S["x1_done"], s.count(1, 1))
                v.bn_stats(st2[:, :], x1).then_inc(S["bn2"], 1)
                dve.wait_ge(S["bn2"], s.count(1, 1))
                v.memset(spare[:, 1:2], 0.0)
                v.bn_aggr(mv2[:, :], st2[:, :]).then_inc(S["mv2_done"], 1)

            def second_norm(s):
                dve.wait_ge(S["rstd2_done"], s.count(1, 1))
                v.tensor_scalar(yn[:, s.buf(2, 2), :], xr[:, s.buf(2, 8), :], mv2[:, 0:1], rstd2[:, 0:1],
                                ALU.subtract, ALU.mult).then_inc(S["yn_done"], 1)

            def y_lo(s):
                dve.wait_ge(S["yT_hi_done"], s.count(1, 1))
                j = (s.q - 2) % GROUP
                half = s.half if s.q >= 2 else 1 - s.half
                cols = slice(j * P, (j + 1) * P)
                v.tensor_tensor(yT_lo[:, half, :, cols], y_ps[:, 0:DIM].rearrange("p (k n) -> p k n", k=KD),
                                yT_hi[:, half, :, cols].bitcast(F32), ALU.subtract).then_inc(S["yT_lo_done"], 1)

            def ffn_event(s, i):
                piece = s.pieces()[i]
                if piece is None:
                    return
                if piece[0] == "D":
                    _, j, part = piece
                    if part:
                        dve.wait_ge(S["down_done"], s.group_count(GROUP, 2, j + 1))
                        pair = GROUP * s.half + j
                        v.scalar_tensor_tensor(out=obuf[:, j, :], in0=ffn_ps[j % 2][:, 0:DIM], scalar=ffn_gate[:, 0:1],
                                               in1=xr[:, pair, :], op0=ALU.mult, op1=ALU.add).then_inc(S["out_ready"], 1)
                    return
                c = piece[1]
                buf = hb[:, c % 2, :]
                if piece[0] == "G":
                    dve.wait_ge(S["tanh_done"], s.group_count(CH, 1, c + 1))
                    v.scalar_tensor_tensor(out=buf, in0=buf, scalar=1.0, in1=ffn_ps[0][:, :],
                                           op0=ALU.add, op1=ALU.mult).then_inc(S["gt_done"], 1)
                else:
                    dve.wait_ge(S["up_done"], s.group_count(2 * CH, 1, 2 * c + 2))
                    dve.wait_ge(S["gt_done"], s.group_count(CH, 1, c + 1))
                    v.tensor_tensor(buf, buf, ffn_ps[1][:, :], ALU.mult).then_inc(S["h_done"], 1)

            for i in range(QKV_PIECES):
                split_weights(i)
            dve.wait_ge(S["tanh_g"], 1)
            v.tensor_scalar(ffn_gate[:, :], tgates[:, 1:2], 0.5, None, ALU.mult).then_inc(S["gate_half"], 1)
            dve.wait_ge(S["gate_half"], 1)

            def emit(s):
                front, back, end = s.has_pair(0), s.has_pair(1), s.has_pair(2)
                if front:
                    first_stats(s)
                ffn_event(s, 0)
                if end:
                    attention_sums(s)
                if front:
                    first_norm(s)
                if end:
                    residual(s)
                if back:
                    p_rest(s, 0)
                if front:
                    t_lo(s)
                if end:
                    second_norm(s)
                if back:
                    p_rest(s, 1)
                ffn_event(s, 1)
                if front:
                    v_rest(s)
                    sums_of_squares(s)
                if back:
                    p_rest(s, 2)
                if end:
                    y_lo(s)
                if front:
                    qk_norm(s)
                if back:
                    p_rest(s, 3)
                ffn_event(s, 2)
                if front:
                    qk_lo(s)
                    lay_out_values(s)
                ffn_event(s, 3)
                ffn_event(s, 4)
                if front:
                    take_q(s)
                ffn_event(s, 5)
                for i in split_in_slot(s):
                    split_weights(i)

            slots(dve, emit)

        @block.gpsimd
        def _(pool):
            g = nc.gpsimd
            g.memset(eps[:, 0:1], LN_EPS)
            g.memset(eps[:, 1:2], RMS_EPS)
            g.memset(ident32[:, :], 0.0).then_inc(S["const_made"], 1)
            g.memset(ident16[:, :], 0.0).then_inc(S["const_made"], 1)
            pool.wait_ge(S["const_made"], 3)
            for ident in (ident32, ident16):
                g.affine_select(out=ident[:, :], in_=ident[:, :], compare_op=ALU.not_equal, fill=1.0, base=0,
                                pattern=[[-1, P]], channel_multiplier=1).then_inc(S["ident_made"], 1)

            def rstd(s, back, mv, ve, r, names):
                got, mid, done = names
                pool.wait_ge(S[got], s.count(1, back - 1))
                g.tensor_tensor(ve[:, :], mv[:, 1:2], eps[:, 0:1], ALU.add).then_inc(S[mid], 1)
                pool.wait_ge(S[mid], s.count(1, back - 1))
                g.tensor_tensor(r[:, :], ve[:, :], neg_half[:, 0:1], ALU.pow).then_inc(S[done], 1)

            def qk_rms(s):
                pool.wait_ge(S["ss_done"], s.count(1, -1))
                g.tensor_tensor(ms[:, :], ss[:, :], eps[:, 1:2].broadcast_to([P, 2 * HEADS]), ALU.add).then_inc(S["ms_done"], 1)
                pool.wait_ge(S["ms_done"], s.count(1, -1))
                g.tensor_tensor(rqk[:, :], ms[:, :], neg_half[:, :], ALU.pow).then_inc(S["rqk_done"], 1)

            def v3_and_qk_hi(s):
                pool.wait_ge(S["norm_done"], s.count(1, -1))
                pool.wait_ge(S["v2_done"], s.count(1, -1))
                g.tensor_tensor(vn[:, :, 0, :], vrem[:, :].rearrange("p (h d) -> p h d", d=HD), vn[:, :, 2, :],
                                ALU.subtract).then_inc(S["v3_done"], 1)
                qk = qk32[:, :].rearrange("p (w h d) -> p w h d", w=2, d=HD)
                for w, (rows, slots_) in enumerate(((q4, slice(0, 2)), (k4, slice(0, 4, 2)))):
                    g.tensor_copy(rows[:, :, slots_, :],
                                  qk[:, w, :, :].unsqueeze(2).broadcast_to([P, HEADS, 2, HD])).then_inc(S["hi_qk"], 1)

            def h_rest(s, i):
                piece = s.pieces()[i]
                if piece is None or piece[0] != "U":
                    return
                c = piece[1]
                pool.wait_ge(S["h_hi_done"], s.group_count(CH, 1, c + 1))
                g.tensor_tensor(h_lo[:, c, :], hb[:, c % 2, :], h_hi[:, c, :].bitcast(F32), ALU.subtract).then_inc(S["h_lo_done"], 1)

            def emit(s):
                if s.has_pair(0):
                    rstd(s, 0, mv1, ve1, rstd1, ("mv1_done", "ve1_done", "rstd1_done"))
                if s.has_pair(2):
                    rstd(s, 2, mv2, ve2, rstd2, ("mv2_done", "ve2_done", "rstd2_done"))
                h_rest(s, 1)
                if s.has_pair(0):
                    qk_rms(s)
                    v3_and_qk_hi(s)
                h_rest(s, 3)
                h_rest(s, 5)

            slots(pool, emit)


def kernel(x, ctx_2048, g_xattn, g_ffn, L0_xattn_Wq, L0_xattn_Wk, L0_xattn_Wv,
           L0_ffn_w_gate, L0_ffn_w_up, L0_ffn_w_down):
    import numpy as np
    import concourse.bacc as bacc
    from concourse.bass_utils import run_bass_kernel_spmd

    kv = np.concatenate([np.asarray(L0_xattn_Wk), np.asarray(L0_xattn_Wv)], axis=0)
    w_qkv = np.concatenate([np.asarray(L0_xattn_Wq), kv[0::2], kv[1::2]], axis=0).T
    w_up = np.concatenate([np.asarray(L0_ffn_w_gate), np.asarray(L0_ffn_w_up)], axis=0).T
    arrays = {
        "x": x, "ctx_in": ctx_2048, "g_attn": g_xattn, "g_ffn": g_ffn,
        "w_qkv": w_qkv, "w_up": w_up, "w_down": np.asarray(L0_ffn_w_down).T,
    }
    nc = bacc.Bacc("TRN2", target_bir_lowering=False, num_devices=1)
    args = []
    for name, a in arrays.items():
        a = arrays[name] = np.ascontiguousarray(a)
        args.append(nc.dram_tensor(name, a.shape, mybir.dt.from_np(a.dtype), kind="ExternalInput").ap())
    args.append(nc.dram_tensor("out", (BATCH, SEQ, DIM), F32, kind="ExternalOutput").ap())
    flamingo_block(nc, *args)
    r = run_bass_kernel_spmd(nc, [arrays], core_ids=[0])
    return r.results[0]["out"]
```

```python
import concourse.bass as bass
from concourse import mybir
from contextlib import ExitStack

F32 = mybir.dt.float32
F32R = mybir.dt.float32r
F16 = mybir.dt.float16
BF16 = mybir.dt.bfloat16
I32 = mybir.dt.int32
ALU = mybir.AluOpType
ACT = mybir.ActivationFunctionType
AX = mybir.AxisListType

BATCH, SEQ, DIM = 64, 64, 256
HEADS, HD = 32, 8
HIDDEN = 1024
P = 128
PAIRS = BATCH * SEQ // P
GROUP = 4
GROUPS = PAIRS // GROUP
KD = DIM // P
CH = HIDDEN // P
RND = 4
TPR = HEADS // 2 // RND
GRP_T = 8
VW = 3 * HD + 1
LN_EPS, RMS_EPS = 1e-5, 1e-6
RSQRT_BITS = float(0x5F3759DF - (1 << 22))
POOL_ROUNDS = (3,)
DVE_ROUNDS = tuple(r for r in range(RND) if r not in POOL_ROUNDS)
NEWTON = 3
SCALE = float(HD) ** -0.5

FFN_PIECES = [
    [("D", 0, 0), ("D", 0, 1), ("D", 1, 0), ("D", 1, 1), ("D", 2, 0), ("D", 2, 1)],
    [("D", 3, 0), ("D", 3, 1), ("G", 0), ("U", 0), ("G", 1), ("U", 1)],
    [("G", 2), ("U", 2), ("G", 3), ("U", 3), ("G", 4), ("U", 4)],
    [("G", 5), ("U", 5), ("G", 6), ("U", 6), ("G", 7), ("U", 7)],
]


class Step:

    def __init__(self, turn, half, q, looped):
        self.turn, self.half, self.q, self.looped = turn, half, q, looped
        self.grp = turn * 2 + half

    def back(self, n):
        place = GROUP * self.half + self.q - n
        turns, place = divmod(place, 2 * GROUP)
        return Step(self.turn + turns if turns else self.turn, place // GROUP, place % GROUP, self.looped)

    def exists(self):
        return self.looped or 0 <= GROUP * self.grp + self.q < PAIRS

    def done(self, back=0, per=1):
        return self.grp * (GROUP * per) + per * (self.q - back + 1)

    def part(self, n, per=RND):
        return self.grp * (GROUP * per) + (per * self.q + n)

    def group_count(self, per_group, back, extra=0):
        return self.grp * per_group + (extra - per_group * back)

    def ring(self, n):
        return (GROUP * self.half + self.q) % n

    def pieces(self):
        out = []
        for piece in FFN_PIECES[self.q]:
            back = 2 if piece[0] == "D" else 1
            ok = self.looped or 0 <= self.grp - back < GROUPS
            out.append(piece if ok else None)
        return out


def slots(eng, emit):
    two_groups = [(half, q) for half in range(2) for q in range(GROUP)]
    for half, q in two_groups:
        emit(Step(0, half, q, False))
    with eng.Fori(1, GROUPS // 2) as turn:
        for half, q in two_groups:
            emit(Step(turn, half, q, True))
    for half, q in two_groups[:GROUP + 3]:
        emit(Step(GROUPS // 2, half, q, False))


def run(work, pair, *more):
    if pair.exists():
        work(pair, *more)


def head_pair(r, tt):
    return 2 * (TPR * (r // 2) + tt) + r % 2


def wait(eng, sem, value):
    if not isinstance(value, int) or value > 0:
        eng.wait_ge(sem, value)


def flamingo_block(nc, x, ctx_in, g_attn, g_ffn, w_qkv, w_up, w_down, out):
    x_t = x.rearrange("(i t b) s d -> i t (b s) d", b=P // SEQ, t=2 * GROUP)
    c_t = ctx_in.rearrange("(i t b) s d -> i t (b s) d", b=P // SEQ, t=2 * GROUP)
    out_g = out.rearrange("(i g t b) s d -> i g (b s) t d", b=P // SEQ, t=GROUP, g=2)
    wqkv_d = w_qkv.rearrange("(k p) n -> p k n", p=P)
    wup_d = w_up.rearrange("(k p) n -> p k n", p=P)
    wdn_d = w_down.rearrange("(k p) n -> p k n", p=P)

    stack = ExitStack()
    with stack:
        def sb(name, shape, dt=F32):
            return stack.enter_context(nc.sbuf_tensor(name, shape, dt))

        def sem(name):
            return stack.enter_context(nc.semaphore(name))

        wqkv_hi, wqkv_lo = (sb(f"wqkv_{n}", [P, KD, 3 * DIM], F32R) for n in ("hi", "lo"))
        wup_hi, wup_lo = (sb(f"wup_{n}", [P, KD, 2 * HIDDEN], F32R) for n in ("hi", "lo"))
        wdn_hi, wdn_lo = (sb(f"wdn_{n}", [P, CH, DIM], F32R) for n in ("hi", "lo"))
        stage = sb("stage", [P, 2, 1024])
        ident32 = sb("ident32", [P, P])
        ident16 = sb("ident16", [P, P], F16)
        neg_half = sb("neg_half", [P, 1])
        one_and_half = sb("one_and_half", [P, 1])
        eps = sb("eps", [P, 1])
        gates = sb("gates", [P, 2])
        tgates = sb("tgates", [P, 2])
        ffn_gate = sb("ffn_gate", [P, 1])

        xbuf = sb("xbuf", [P, 4, DIM])
        cbuf = sb("cbuf", [P, 4, DIM])
        st1, mv1, ve1, rstd1 = sb("st1", [P, 6]), sb("mv1", [P, 2]), sb("ve1", [P, 1]), sb("rstd1", [P, 1])
        st2, mv2, ve2, rstd2 = sb("st2", [P, 6]), sb("mv2", [P, 2]), sb("ve2", [P, 1]), sb("rstd2", [P, 1])
        spare = sb("spare", [P, 2])
        xn = sb("xn", [P, 2, DIM])
        tT_hi, tT_lo = (sb(f"tT_{n}", [P, 2 * KD, P], F32R) for n in ("hi", "lo"))
        sq = sb("sq", [P, 2 * DIM])
        ss, half_ms, rqk, nt = (sb(n, [P, 2 * HEADS]) for n in ("ss", "half_ms", "rqk", "nt"))
        qk32 = sb("qk32", [P, 2 * DIM])
        q4 = sb("q4", [P, HEADS, 4, HD], F16)
        k4 = sb("k4", [P, HEADS, 4, HD], F16)
        qT = sb("qT", [P, GRP_T, 2, SEQ], F16)
        kT = sb("kT", [P, GRP_T, 2, 2, SEQ], F16)
        parity = sb("parity", [P, 2])
        vrem = sb("vrem", [P, DIM])
        vn = sb("vn", [P, HEADS, 3, HD], BF16)
        vp_flat = sb("vp", [P, 4 * HEADS * VW], BF16)
        vp = vp_flat[:, :].rearrange("p (u t b a c) -> p u t b a c", u=2, b=2, a=2, c=VW)
        p32 = sb("p32", [P, RND, 512])
        p_hi = sb("p_hi", [P, RND, 512], F16)
        p_lo = sb("p_lo", [P, RND, 512], F16)
        oa = sb("oa", [P, HEADS, VW])
        asum = sb("asum", [P, DIM])
        rinv = sb("rinv", [P, HEADS])
        xr = sb("xr", [P, 8, DIM])
        yn = sb("yn", [P, 2, DIM])
        yT_hi, yT_lo = (sb(f"yT_{n}", [P, 2, KD, 512], F32R) for n in ("hi", "lo"))
        hb = sb("hb", [P, 3, 512])
        h_hi, h_lo = (sb(f"h_{n}", [P, CH, 512], F32R) for n in ("hi", "lo"))
        obuf = sb("obuf", [P, GROUP, DIM])

        bank = [stack.enter_context(nc.psum_tensor(f"bank{i}", [P, 512], F32)) for i in range(8)]
        ffn_ps = bank[0:3]
        tr_ps, qk_ps, o_ps = bank[3:6]
        s_ps = bank[6:8]
        v_ps = tr_ps[:, 0:DIM]
        y_ps = tr_ps[:, DIM:2 * DIM]
        qT_ps, kT_ps = (b[:, :].bitcast(F16) for b in s_ps)

        def ffn_bank(piece):
            kind, n = piece[0], piece[1]
            return ffn_ps[(n if kind == "D" else GROUP + 2 * n + (kind == "U")) % 3]

        names = """x_in0 x_in1 x_in2 x_in3 c_in0 c_in1 c_in2 c_in3 w_in0 w_in1 gate_in out_stored
            zeroed parity_made ident_made const_made w_hi w_lo tanh_g gate_half
            bn1 mv1_done ve1_done rstd1_done xn_done tr_done tT_hi_done tT_lo_done qk_done v_done
            sq_done ss_done half_ms_done seeded newton nt1 nt2 nt3 norm_done hi_qk lo_qk qT_tr kT_tr qT_done kT_done
            v1_done vrem_done v2_done v3_done vp_done s_done p32_done p_hi_done p_lo_done p_lo_pool pv_done
            o_done asum_done rinv_done attn_done x1_done bn2 mv2_done ve2_done rstd2_done yn_done
            y_tr yT_hi_done yT_lo_done up_done tanh_done gt_done h_done h_hi_done h_lo_done
            down_done out_ready""".split()
        S = {n: sem(n) for n in names}
        x_in = [S[f"x_in{i}"] for i in range(4)]
        c_in = [S[f"c_in{i}"] for i in range(4)]
        w_in = [S[f"w_in{i}"] for i in range(2)]

        pieces = [(wqkv_d[:, k, :], wqkv_hi[:, k, :], wqkv_lo[:, k, :]) for k in range(KD)]
        for k in range(KD):
            for u in range(2):
                c = slice(u * HIDDEN, (u + 1) * HIDDEN)
                pieces.append((wup_d[:, k, c], wup_hi[:, k, c], wup_lo[:, k, c]))
        for u in range(2):
            c = slice(4 * u, 4 * u + 4)
            flat = "p k n -> p (k n)"
            pieces.append((wdn_d[:, c, :], wdn_hi[:, c, :].rearrange(flat), wdn_lo[:, c, :].rearrange(flat)))
        QKV_PIECES, UP_PIECES = KD, 3 * KD

        def staged(i):
            return stage[:, i % 2, 0:pieces[i][1].shape[1]]

        def split_in_slot(s):
            if s.looped or s.grp > 0 or not 1 <= s.q <= 3:
                return []
            return [QKV_PIECES + 2 * s.q - 2, QKV_PIECES + 2 * s.q - 1]

        block = stack.enter_context(nc.Block())

        @block.sync
        def _(sp):
            def load_weights(i):
                if i >= 2:
                    sp.wait_ge(S["w_lo"], i - 1)
                dst = staged(i)
                if i >= UP_PIECES:
                    dst = dst.rearrange("p (k n) -> p k n", n=DIM)
                sp.dma_start(dst, pieces[i][0]).then_inc(w_in[i % 2], 16)

            def load_pair(s):
                pair = GROUP * s.half + s.q
                wait(sp, S["x1_done"], s.done(4))
                sp.dma_start(xbuf[:, s.q, :], x_t[s.turn, pair, :, :]).then_inc(x_in[s.q], 16)
                sp.dma_start(cbuf[:, s.q, :], c_t[s.turn, pair, :, :]).then_inc(c_in[s.q], 16)

            load_pair(Step(0, 0, 0, False))
            load_weights(0)
            load_weights(1)
            for q in range(1, GROUP):
                load_pair(Step(0, 0, q, False))
            for col, g in enumerate((g_attn, g_ffn)):
                sp.dma_start(gates[:, col:col + 1], g.partition_broadcast(P)).then_inc(S["gate_in"], 16)
            for i in range(2, len(pieces)):
                load_weights(i)
            for q in range(GROUP):
                load_pair(Step(0, 1, q, False))
            with sp.Fori(1, GROUPS // 2) as turn:
                for half in range(2):
                    for q in range(GROUP):
                        load_pair(Step(turn, half, q, True))

        @block.tensor
        def _(pe):
            mm = nc.tensor.matmul

            def product(o, left, right, first, last):
                (lh, ll), (rh, rl) = left, right
                mm(o, lh, rh, start=first, stop=False)
                mm(o, lh, rl, start=False, stop=False)
                return mm(o, ll, rh, start=False, stop=last)

            def transposes(s):
                pe.wait_ge(c_in[s.q], s.group_count(16, -1))
                wait(pe, S["vrem_done"], s.done(1))
                wait(pe, S["yT_lo_done"], s.done(3))
                pe.wait_ge(S["xn_done"], s.done())
                for k in range(KD):
                    nc.tensor.transpose(tr_ps[:, k * P:(k + 1) * P], xn[:, s.ring(2), k * P:(k + 1) * P],
                                        ident32[:, :])
                for k in range(KD):
                    last = nc.tensor.transpose(tr_ps[:, (KD + k) * P:(KD + k + 1) * P],
                                               cbuf[:, s.q, k * P:(k + 1) * P], ident32[:, :])
                last.then_inc(S["tr_done"], 1)

            def project(s):
                if not s.looped:
                    pe.wait_ge(S["w_lo"], QKV_PIECES)
                pe.wait_ge(S["tT_hi_done"], s.done())
                pe.wait_ge(S["tT_lo_done"], s.done())

                def one(o, part, col):
                    for k in range(KD):
                        last = product(o, (tT_hi[:, KD * part + k, :], tT_lo[:, KD * part + k, :]),
                                       (wqkv_hi[:, k, col:col + DIM], wqkv_lo[:, k, col:col + DIM]),
                                       k == 0, k == KD - 1)
                    return last

                one(v_ps, 1, 2 * DIM).then_inc(S["v_done"], 1)
                wait(pe, S["norm_done"], s.done(1))
                one(qk_ps[:, 0:DIM], 0, 0)
                one(qk_ps[:, DIM:2 * DIM], 1, DIM).then_inc(S["qk_done"], 1)

            def qk_transposes(s):
                pe.wait_ge(S["lo_qk"], s.done())
                wait(pe, S["p_hi_done"], s.done(1, RND))
                q_rows = q4[:, :, :, :].rearrange("p (g h) c d -> p g (h c d)", g=GRP_T)
                k_rows = k4[:, :, :, :].rearrange("p (g h) c d -> p g (h c d)", g=GRP_T)
                for rows, ps, done in ((q_rows, qT_ps, "qT_tr"), (k_rows, kT_ps, "kT_tr")):
                    for g in range(GRP_T):
                        last = nc.tensor.transpose(ps[:, g * P:(g + 1) * P], rows[:, g, :], ident16[:, :])
                    last.then_inc(S[done], 1)

            def scores(s, r):
                if r == 0:
                    pe.wait_ge(S["qT_done"], s.done())
                    pe.wait_ge(S["kT_done"], s.done())
                if r >= 2:
                    pe.wait_ge(S["p_hi_done"], s.part(r - 1))
                o = s_ps[r % 2][:, :].rearrange("p (t b n) -> p t b n", t=TPR, b=2)
                rows = slice(SEQ * (r % 2), SEQ * (r % 2) + SEQ)
                for tt in range(TPR):
                    g = TPR * (r // 2) + tt
                    for b in range(2):
                        last = mm(o[:, tt, b, :], kT[rows, g, b, :, :].rearrange("p a m -> p (a m)"), qT[rows, g, b, :], start=True, stop=True)
                last.then_inc(S["s_done"], 1)

            def attend(s, r):
                if r == 0:
                    pe.wait_ge(S["vp_done"], s.done())
                wait(pe, S["o_done"], s.part(r))
                if r in POOL_ROUNDS:
                    pe.wait_ge(S["p_lo_pool"], s.part(POOL_ROUNDS.index(r) + 1, len(POOL_ROUNDS)))
                else:
                    pe.wait_ge(S["p_lo_done"], s.part(DVE_ROUNDS.index(r) + 1, len(DVE_ROUNDS)))
                o = o_ps[:, 0:TPR * 4 * VW].rearrange("p (t c) -> p t c", t=TPR)
                for tt in range(TPR):
                    values = vp[:, s.ring(2), head_pair(r, tt), :, :, :].rearrange("p b a c -> p (b a) c")
                    cols = slice(tt * P, (tt + 1) * P)
                    mm(o[:, tt, :], p_hi[:, r, cols], values.rearrange("p a c -> p (a c)"), start=True, stop=False)
                    last = mm(o[:, tt, :].rearrange("p (a c) -> p a c", c=VW)[:, :, HD:VW],
                              p_lo[:, r, cols], values[:, :, HD:VW], start=False, stop=True)
                last.then_inc(S["pv_done"], 1)

            def y_transposes(s):
                pe.wait_ge(S["yn_done"], s.done())
                pe.wait_ge(S["vrem_done"], s.done(-2) if s.back(-2).exists() else PAIRS)
                for k in range(KD):
                    last = nc.tensor.transpose(y_ps[:, k * P:(k + 1) * P], yn[:, s.ring(2), k * P:(k + 1) * P],
                                               ident32[:, :])
                last.then_inc(S["y_tr"], 1)

            def ffn_piece(s, i):
                piece = s.pieces()[i]
                if piece is None:
                    return
                if piece[0] == "D":
                    _, j, part = piece
                    if (j, part) == (0, 0):
                        pe.wait_ge(S["h_hi_done"], s.group_count(CH, 1))
                        pe.wait_ge(S["h_lo_done"], s.group_count(CH, 1))
                        if not s.looped:
                            pe.wait_ge(S["w_lo"], len(pieces))
                    if j >= 3 and part == 0:
                        pe.wait_ge(S["out_ready"], s.group_count(GROUP, 2, j - 2))
                    o = ffn_bank(piece)[:, 0:DIM]
                    tok = slice(j * P, (j + 1) * P)
                    for c in range(CH // 2 * part, CH // 2 * (part + 1)):
                        last = product(o, (h_hi[:, c, tok], h_lo[:, c, tok]), (wdn_hi[:, c, :], wdn_lo[:, c, :]),
                                       c == 0, c == CH - 1)
                    if part:
                        last.then_inc(S["down_done"], 1)
                    return
                up, c = piece[0] == "U", piece[1]
                if c == 0 and not up:
                    pe.wait_ge(S["yT_hi_done"], s.group_count(GROUP, 0))
                    pe.wait_ge(S["yT_lo_done"], s.group_count(GROUP, 0))
                    if not s.looped:
                        pe.wait_ge(S["w_lo"], UP_PIECES)
                n = 2 * c + up
                if n < 3:
                    wait(pe, S["out_ready"], s.group_count(GROUP, 2, n + 2) if s.looped or s.grp > 1 else 0)
                elif up:
                    pe.wait_ge(S["gt_done"], s.group_count(CH, 1, c))
                else:
                    pe.wait_ge(S["h_done"], s.group_count(CH, 1, c - 1))
                col = slice(up * HIDDEN + c * P, up * HIDDEN + (c + 1) * P)
                half = 1 - s.half
                for k in range(KD):
                    last = product(ffn_bank(piece)[:, :], (wup_hi[:, k, col], wup_lo[:, k, col]),
                                   (yT_hi[:, half, k, :], yT_lo[:, half, k, :]), k == 0, k == KD - 1)
                last.then_inc(S["up_done"], 1)

            pe.wait_ge(S["ident_made"], 2)
            pe.wait_ge(S["zeroed"], 2)

            def emit(s):
                run(qk_transposes, s.back(2))
                run(project, s.back(1))
                ffn_piece(s.back(1), 0)
                run(scores, s.back(2), 0)
                run(scores, s.back(2), 1)
                ffn_piece(s.back(1), 1)
                run(y_transposes, s.back(3))
                run(attend, s.back(2), 0)
                run(scores, s.back(2), 2)
                ffn_piece(s.back(1), 2)
                run(scores, s.back(2), 3)
                run(attend, s.back(2), 1)
                ffn_piece(s.back(1), 3)
                run(attend, s.back(2), 2)
                run(transposes, s)
                ffn_piece(s.back(1), 4)
                run(attend, s.back(2), 3)
                ffn_piece(s.back(1), 5)

            slots(pe, emit)

        @block.scalar
        def _(act):
            def split_weights(i):
                act.wait_ge(w_in[i % 2], 16 * (i // 2 + 1))
                nc.scalar.activation(pieces[i][1], staged(i), ACT.Copy).then_inc(S["w_hi"], 1)

            def split_more(s):
                for i in split_in_slot(s):
                    split_weights(i)

            def exps(s, r):
                act.wait_ge(S["s_done"], s.part(r + 1))
                nc.scalar.activation(p32[:, r, :], s_ps[r % 2][:, :], ACT.Exp, scale=SCALE).then_inc(S["p32_done"], 1)
                nc.scalar.activation(p_hi[:, r, :], s_ps[r % 2][:, :], ACT.Exp, scale=SCALE).then_inc(S["p_hi_done"], 1)

            def t_hi(s):
                act.wait_ge(S["tr_done"], s.done())
                nc.scalar.activation(tT_hi[:, :, :].rearrange("p k n -> p (k n)"), tr_ps[:, :],
                                     ACT.Copy).then_inc(S["tT_hi_done"], 1)

            def v_first(s):
                act.wait_ge(S["v_done"], s.done())
                wait(act, S["vp_done"], s.done(1))
                nc.scalar.activation(vn[:, :, 1, :], v_ps.rearrange("p (h d) -> p h d", d=HD),
                                     ACT.Copy).then_inc(S["v1_done"], 1)

            def squares(s):
                act.wait_ge(S["qk_done"], s.done())
                nc.scalar.activation(sq[:, :], qk_ps[:, :], ACT.Square, scale=float(HD) ** -0.5).then_inc(S["sq_done"], 1)

            def v_second(s):
                act.wait_ge(S["vrem_done"], s.done())
                nc.scalar.activation(vn[:, :, 2, :], vrem[:, :].rearrange("p (h d) -> p h d", d=HD),
                                     ACT.Copy).then_inc(S["v2_done"], 1)

            def y_hi(s):
                act.wait_ge(S["y_tr"], s.done())
                nc.scalar.activation(yT_hi[:, s.half, :, s.q * P:(s.q + 1) * P],
                                     y_ps.rearrange("p (k n) -> p k n", k=KD),
                                     ACT.Copy).then_inc(S["yT_hi_done"], 1)

            def take_k(s):
                act.wait_ge(S["kT_tr"], s.done())
                for a in range(2):
                    last = nc.scalar.activation(kT[:, :, :, a, :], kT_ps[:, :].rearrange("p (g b m) -> p g b m", b=2, m=SEQ),
                                                ACT.Copy, scale=parity[:, a:a + 1])
                last.then_inc(S["kT_done"], 1)

            def take_o(s, r):
                act.wait_ge(S["pv_done"], s.part(r + 1))
                if r == 0:
                    wait(act, S["rinv_done"], s.done(1))
                for b in range(2):
                    rows = slice(SEQ * b, SEQ * (b + 1))
                    o = o_ps[rows, 0:TPR * 4 * VW].rearrange("p (t b c) -> p t b c", t=TPR, b=2)
                    to = oa[rows, :, :].rearrange("p (g u a) c -> p g u (a c)", u=2, a=2)
                    g = TPR * (r // 2)
                    last = nc.scalar.activation(to[:, g:g + TPR, r % 2, :], o[:, :, b, :], ACT.Copy)
                last.then_inc(S["o_done"], 1)

            def ffn_event(s, i):
                piece = s.pieces()[i]
                if piece is None or piece[0] == "D":
                    return
                c = piece[1]
                if piece[0] == "G":
                    act.wait_ge(S["up_done"], s.group_count(2 * CH, 1, 2 * c + 1))
                    wait(act, S["h_lo_done"], s.group_count(CH, 1, max(c - 2, 0)))
                    nc.scalar.activation(hb[:, c % 3, :], ffn_bank(piece)[:, :], ACT.Tanh,
                                         scale=0.5).then_inc(S["tanh_done"], 1)
                else:
                    act.wait_ge(S["h_done"], s.group_count(CH, 1, c + 1))
                    nc.scalar.activation(h_hi[:, c, :], hb[:, c % 3, :], ACT.Copy).then_inc(S["h_hi_done"], 1)

            def store_out(s):
                if s.looped or s.grp >= 2:
                    if s.q == 1:
                        act.wait_ge(S["out_ready"], s.group_count(GROUP, 1))
                        act.dma_start(out_g[s.turn - 1, s.half, :, :, :], obuf[:, :, :]).then_inc(S["out_stored"], 16)
                    elif s.q == 2:
                        act.wait_ge(S["out_stored"], s.group_count(16, 1))

            for i in range(QKV_PIECES):
                split_weights(i)
            act.wait_ge(S["gate_in"], 32)
            nc.scalar.activation(tgates[:, :], gates[:, :], ACT.Tanh).then_inc(S["tanh_g"], 1)

            def emit(s):
                run(squares, s.back(1))
                run(v_first, s.back(1))
                ffn_event(s.back(1), 0)
                run(exps, s.back(2), 0)
                run(v_second, s.back(1))
                run(exps, s.back(2), 1)
                run(y_hi, s.back(3))
                run(take_o, s.back(2), 0)
                run(exps, s.back(2), 2)
                ffn_event(s.back(1), 2)
                run(take_o, s.back(2), 1)
                ffn_event(s.back(1), 1)
                run(exps, s.back(2), 3)
                run(t_hi, s)
                ffn_event(s.back(1), 3)
                run(take_o, s.back(2), 2)
                ffn_event(s.back(1), 4)
                run(take_o, s.back(2), 3)
                split_more(s)
                ffn_event(s.back(1), 5)
                store_out(s.back(1))
                run(take_k, s.back(1))

            act.wait_ge(S["parity_made"], 2)
            slots(act, emit)
            act.wait_ge(S["out_stored"], 16 * GROUPS)

        @block.vector
        def _(dve):
            v = nc.vector
            v.memset(parity[:, :], 0.0).then_inc(S["parity_made"], 1)
            dve.wait_ge(S["parity_made"], 1)
            for j in range(4):
                last = v.memset(parity[32 * j:32 * j + 32, j % 2:j % 2 + 1], 1.0)
            last.then_inc(S["parity_made"], 1)
            v.memset(one_and_half[:, :], 1.5)
            v.memset(neg_half[:, :], -0.5).then_inc(S["const_made"], 1)
            v.memset(vp_flat[:, :].bitcast(F32), 0.0).then_inc(S["zeroed"], 1)
            dve.wait_ge(S["zeroed"], 1)
            for a in range(2):
                last = v.memset(vp[SEQ * a:SEQ * (a + 1), :, :, :, a, 3 * HD:VW], 1.0)
            last.then_inc(S["zeroed"], 1)

            def split_weights(i):
                dve.wait_ge(S["w_hi"], i + 1)
                v.tensor_tensor(pieces[i][2], staged(i), pieces[i][1].bitcast(F32), ALU.subtract).then_inc(S["w_lo"], 1)

            def split_more(s):
                for i in split_in_slot(s):
                    split_weights(i)

            def first_stats(s):
                dve.wait_ge(x_in[s.q], s.group_count(16, -1))
                v.bn_stats(st1[:, :], xbuf[:, s.q, :]).then_inc(S["bn1"], 1)
                dve.wait_ge(S["bn1"], s.done())
                v.memset(spare[:, 0:1], 0.0)
                v.bn_aggr(mv1[:, :], st1[:, :]).then_inc(S["mv1_done"], 1)

            def first_norm(s):
                dve.wait_ge(S["rstd1_done"], s.done())
                v.tensor_scalar(xn[:, s.ring(2), :], xbuf[:, s.q, :], mv1[:, 0:1], rstd1[:, 0:1],
                                ALU.subtract, ALU.mult).then_inc(S["xn_done"], 1)

            def t_lo(s):
                dve.wait_ge(S["tT_hi_done"], s.done())
                flat = "p k n -> p (k n)"
                v.tensor_tensor(tT_lo[:, :, :].rearrange(flat), tr_ps[:, :],
                                tT_hi[:, :, :].rearrange(flat).bitcast(F32), ALU.subtract).then_inc(S["tT_lo_done"], 1)

            def v_rest(s):
                dve.wait_ge(S["v1_done"], s.done())
                v.tensor_tensor(vrem[:, :].rearrange("p (h d) -> p h d", d=HD),
                                v_ps.rearrange("p (h d) -> p h d", d=HD), vn[:, :, 1, :],
                                ALU.subtract).then_inc(S["vrem_done"], 1)

            def sums_of_squares(s):
                dve.wait_ge(S["sq_done"], s.done())
                v.tensor_reduce(ss[:, :], sq[:, :].rearrange("p (h d) -> p h d", d=HD), AX.X, ALU.add).then_inc(S["ss_done"], 1)
                dve.wait_ge(S["ss_done"], s.done())
                v.tensor_scalar(half_ms[:, :], ss[:, :], RMS_EPS, 0.5, ALU.add, ALU.mult).then_inc(S["half_ms_done"], 1)
                dve.wait_ge(S["half_ms_done"], s.done())
                v.tensor_scalar(rqk[:, :].bitcast(I32), half_ms[:, :].bitcast(I32), -0.5, RSQRT_BITS,
                                ALU.mult, ALU.add).then_inc(S["seeded"], 1)

            def qk_norm(s):
                dve.wait_ge(S["newton"], s.done(0, NEWTON))
                v.tensor_tensor(qk32[:, :].rearrange("p (h d) -> p h d", d=HD),
                                qk_ps[:, :].rearrange("p (h d) -> p h d", d=HD),
                                rqk[:, :].unsqueeze(2).broadcast_to([P, 2 * HEADS, HD]), ALU.mult).then_inc(S["norm_done"], 1)

            def qk_parts(s):
                dve.wait_ge(S["norm_done"], s.done())
                qk = qk32[:, :].rearrange("p (w h d) -> p w h d", w=2, d=HD)
                for w, (rows, slots_) in enumerate(((q4, slice(0, 2)), (k4, slice(0, 4, 2)))):
                    v.tensor_copy(rows[:, :, slots_, :],
                                  qk[:, w, :, :].unsqueeze(2).broadcast_to([P, HEADS, 2, HD])).then_inc(S["hi_qk"], 1)
                dve.wait_ge(S["hi_qk"], s.done(0, 2))
                for w, (rows, slots_) in enumerate(((q4, slice(2, 4)), (k4, slice(1, 4, 2)))):
                    hi = rows[:, :, 0, :]
                    last = v.tensor_tensor(rows[:, :, slots_, :], qk[:, w, :, :].unsqueeze(2).broadcast_to([P, HEADS, 2, HD]),
                                           hi.unsqueeze(2).broadcast_to([P, HEADS, 2, HD]), ALU.subtract)
                last.then_inc(S["lo_qk"], 1)

            def lay_out_values(s):
                dve.wait_ge(S["v3_done"], s.done())
                wait(dve, S["pv_done"], s.done(2, RND))
                for a in range(2):
                    for b in range(2):
                        src = vn[SEQ * b:SEQ * (b + 1), :, :, :].rearrange("p (t a) c d -> p t a (c d)", a=2)
                        last = v.tensor_copy(vp[SEQ * a:SEQ * (a + 1), s.ring(2), :, b, a, 0:3 * HD], src[:, :, a, :])
                last.then_inc(S["vp_done"], 1)

            def p_rest(s, r):
                dve.wait_ge(S["p_hi_done"], s.part(r + 1))
                v.tensor_tensor(p_lo[:, r, :], p32[:, r, :], p_hi[:, r, :], ALU.subtract).then_inc(S["p_lo_done"], 1)

            def attention_sums(s):
                dve.wait_ge(S["o_done"], s.done(0, RND))
                parts = oa[:, :, 0:3 * HD].rearrange("p h (c d) -> p h d c", d=HD)
                v.tensor_reduce(asum[:, :].rearrange("p (h d) -> p h d", d=HD), parts, AX.X, ALU.add).then_inc(S["asum_done"], 1)
                v.reciprocal(rinv[:, :], oa[:, :, 3 * HD]).then_inc(S["rinv_done"], 1)

            def residual(s):
                dve.wait_ge(S["rinv_done"], s.done())
                a3 = asum[:, :].rearrange("p (h d) -> p h d", d=HD)
                v.tensor_tensor(a3, a3, rinv[:, :].unsqueeze(2).broadcast_to([P, HEADS, HD]), ALU.mult).then_inc(S["attn_done"], 1)
                dve.wait_ge(S["attn_done"], s.done())
                x1 = xr[:, s.ring(8), :]
                v.scalar_tensor_tensor(out=x1, in0=asum[:, :], scalar=tgates[:, 0:1], in1=xbuf[:, s.q, :],
                                       op0=ALU.mult, op1=ALU.add).then_inc(S["x1_done"], 1)
                dve.wait_ge(S["x1_done"], s.done())
                v.bn_stats(st2[:, :], x1).then_inc(S["bn2"], 1)
                dve.wait_ge(S["bn2"], s.done())
                v.memset(spare[:, 1:2], 0.0)
                v.bn_aggr(mv2[:, :], st2[:, :]).then_inc(S["mv2_done"], 1)

            def second_norm(s):
                dve.wait_ge(S["rstd2_done"], s.done())
                v.tensor_scalar(yn[:, s.ring(2), :], xr[:, s.ring(8), :], mv2[:, 0:1], rstd2[:, 0:1],
                                ALU.subtract, ALU.mult).then_inc(S["yn_done"], 1)

            def y_lo(s):
                dve.wait_ge(S["yT_hi_done"], s.done())
                cols = slice(s.q * P, (s.q + 1) * P)
                v.tensor_tensor(yT_lo[:, s.half, :, cols], y_ps.rearrange("p (k n) -> p k n", k=KD),
                                yT_hi[:, s.half, :, cols].bitcast(F32), ALU.subtract).then_inc(S["yT_lo_done"], 1)

            def ffn_event(s, i):
                piece = s.pieces()[i]
                if piece is None:
                    return
                if piece[0] == "D":
                    _, j, part = piece
                    if part:
                        dve.wait_ge(S["down_done"], s.group_count(GROUP, 2, j + 1))
                        pair = GROUP * s.half + j
                        v.scalar_tensor_tensor(out=obuf[:, j, :], in0=ffn_bank(piece)[:, 0:DIM], scalar=ffn_gate[:, 0:1],
                                               in1=xr[:, pair, :], op0=ALU.mult, op1=ALU.add).then_inc(S["out_ready"], 1)
                    return
                c = piece[1]
                buf = hb[:, c % 3, :]
                if piece[0] == "G":
                    dve.wait_ge(S["tanh_done"], s.group_count(CH, 1, c + 1))
                    v.scalar_tensor_tensor(out=buf, in0=buf, scalar=1.0, in1=ffn_bank(piece)[:, :],
                                           op0=ALU.add, op1=ALU.mult).then_inc(S["gt_done"], 1)
                else:
                    dve.wait_ge(S["up_done"], s.group_count(2 * CH, 1, 2 * c + 2))
                    dve.wait_ge(S["gt_done"], s.group_count(CH, 1, c + 1))
                    v.tensor_tensor(buf, buf, ffn_bank(piece)[:, :], ALU.mult).then_inc(S["h_done"], 1)

            for i in range(QKV_PIECES):
                split_weights(i)
            dve.wait_ge(S["tanh_g"], 1)
            v.tensor_scalar(ffn_gate[:, :], tgates[:, 1:2], 0.5, None, ALU.mult).then_inc(S["gate_half"], 1)
            dve.wait_ge(S["gate_half"], 1)

            def take_q(s):
                dve.wait_ge(S["qT_tr"], s.done())
                v.tensor_copy(qT[:, :, :, :].rearrange("p g b n -> p (g b n)"), qT_ps[:, :]).then_inc(S["qT_done"], 1)

            def emit(s):
                run(attention_sums, s.back(3))
                run(residual, s.back(3))
                run(take_q, s.back(2))
                run(first_stats, s)
                run(second_norm, s.back(3))
                run(v_rest, s.back(1))
                run(sums_of_squares, s.back(1))
                run(first_norm, s)
                ffn_event(s.back(1), 0)
                run(p_rest, s.back(2), 0)
                ffn_event(s.back(1), 1)
                run(y_lo, s.back(3))
                run(p_rest, s.back(2), 1)
                run(lay_out_values, s.back(1))
                ffn_event(s.back(1), 2)
                run(p_rest, s.back(2), 2)
                run(qk_norm, s.back(1))
                ffn_event(s.back(1), 3)
                run(qk_parts, s.back(1))
                ffn_event(s.back(1), 4)
                run(t_lo, s)
                split_more(s)
                ffn_event(s.back(1), 5)

            slots(dve, emit)

        @block.gpsimd
        def _(pool):
            g = nc.gpsimd
            g.memset(eps[:, :], LN_EPS)
            g.memset(ident32[:, :], 0.0).then_inc(S["const_made"], 1)
            g.memset(ident16[:, :], 0.0).then_inc(S["const_made"], 1)
            pool.wait_ge(S["const_made"], 3)
            for ident in (ident32, ident16):
                g.affine_select(out=ident[:, :], in_=ident[:, :], compare_op=ALU.not_equal, fill=1.0, base=0,
                                pattern=[[-1, P]], channel_multiplier=1).then_inc(S["ident_made"], 1)

            def rstd(s, mv, ve, r, n):
                got, mid, done = (name + n + "_done" for name in ("mv", "ve", "rstd"))
                pool.wait_ge(S[got], s.done())
                g.tensor_tensor(ve[:, :], mv[:, 1:2], eps[:, 0:1], ALU.add).then_inc(S[mid], 1)
                pool.wait_ge(S[mid], s.done())
                g.tensor_tensor(r[:, :], ve[:, :], neg_half[:, 0:1], ALU.pow).then_inc(S[done], 1)

            def newton(s, n):
                if n == 0:
                    pool.wait_ge(S["seeded"], s.done())
                else:
                    pool.wait_ge(S["newton"], s.part(n, NEWTON))
                g.tensor_tensor(nt[:, :], half_ms[:, :], rqk[:, :], ALU.mult).then_inc(S["nt1"], 1)
                pool.wait_ge(S["nt1"], s.part(n + 1, NEWTON))
                g.tensor_tensor(nt[:, :], nt[:, :], rqk[:, :], ALU.mult).then_inc(S["nt2"], 1)
                pool.wait_ge(S["nt2"], s.part(n + 1, NEWTON))
                g.tensor_tensor(nt[:, :], one_and_half[:, 0:1].broadcast_to([P, 2 * HEADS]), nt[:, :],
                                ALU.subtract).then_inc(S["nt3"], 1)
                pool.wait_ge(S["nt3"], s.part(n + 1, NEWTON))
                g.tensor_tensor(rqk[:, :], rqk[:, :], nt[:, :], ALU.mult).then_inc(S["newton"], 1)

            def v_third(s):
                pool.wait_ge(S["v2_done"], s.done())
                g.tensor_tensor(vn[:, :, 0, :], vrem[:, :].rearrange("p (h d) -> p h d", d=HD), vn[:, :, 2, :],
                                ALU.subtract).then_inc(S["v3_done"], 1)

            def h_rest(s, i):
                piece = s.pieces()[i]
                if piece is None or piece[0] != "U":
                    return
                c = piece[1]
                pool.wait_ge(S["h_hi_done"], s.group_count(CH, 1, c + 1))
                g.tensor_tensor(h_lo[:, c, :], hb[:, c % 3, :], h_hi[:, c, :].bitcast(F32), ALU.subtract).then_inc(S["h_lo_done"], 1)

            def p_rest(s, r):
                pool.wait_ge(S["p_hi_done"], s.part(r + 1))
                g.tensor_tensor(p_lo[:, r, :], p32[:, r, :], p_hi[:, r, :], ALU.subtract).then_inc(S["p_lo_pool"], 1)

            def emit(s):
                run(rstd, s, mv1, ve1, rstd1, "1")
                run(newton, s.back(1), 0)
                run(v_third, s.back(1))
                run(newton, s.back(1), 1)
                run(newton, s.back(1), 2)
                h_rest(s.back(1), 1)
                run(p_rest, s.back(2), 3)
                h_rest(s.back(1), 3)
                h_rest(s.back(1), 5)
                run(rstd, s.back(2), mv2, ve2, rstd2, "2")

            slots(pool, emit)


def kernel(x, ctx_2048, g_xattn, g_ffn, L0_xattn_Wq, L0_xattn_Wk, L0_xattn_Wv,
           L0_ffn_w_gate, L0_ffn_w_up, L0_ffn_w_down):
    import numpy as np
    import concourse.bacc as bacc
    from concourse.bass_utils import run_bass_kernel_spmd

    kv = np.concatenate([np.asarray(L0_xattn_Wk), np.asarray(L0_xattn_Wv)], axis=0)
    w_qkv = np.concatenate([np.asarray(L0_xattn_Wq), kv[0::2], kv[1::2]], axis=0).T
    w_up = np.concatenate([np.asarray(L0_ffn_w_gate), np.asarray(L0_ffn_w_up)], axis=0).T
    arrays = {
        "x": x, "ctx_in": ctx_2048, "g_attn": g_xattn, "g_ffn": g_ffn,
        "w_qkv": w_qkv, "w_up": w_up, "w_down": np.asarray(L0_ffn_w_down).T,
    }
    nc = bacc.Bacc("TRN2", target_bir_lowering=False, num_devices=1)
    args = []
    for name, a in arrays.items():
        a = arrays[name] = np.ascontiguousarray(a)
        args.append(nc.dram_tensor(name, a.shape, mybir.dt.from_np(a.dtype), kind="ExternalInput").ap())
    args.append(nc.dram_tensor("out", (BATCH, SEQ, DIM), F32, kind="ExternalOutput").ap())
    flamingo_block(nc, *args)
    r = run_bass_kernel_spmd(nc, [arrays], core_ids=[0])
    return r.results[0]["out"]
```

```python
import concourse.bass as bass
from concourse import mybir
from contextlib import ExitStack

F32 = mybir.dt.float32
F32R = mybir.dt.float32r
F16 = mybir.dt.float16
BF16 = mybir.dt.bfloat16
I32 = mybir.dt.int32
ALU = mybir.AluOpType
ACT = mybir.ActivationFunctionType
AX = mybir.AxisListType

BATCH, SEQ, DIM = 64, 64, 256
HEADS, HD = 32, 8
HIDDEN = 1024
P = 128
PAIRS = BATCH * SEQ // P
GROUP = 4
GROUPS = PAIRS // GROUP
KD = DIM // P
CH = HIDDEN // P
RND = 4
TPR = HEADS // 2 // RND
GRP_T = 8
VW = 3 * HD + 1
LN_EPS, RMS_EPS = 1e-5, 1e-6
RSQRT_BITS = float(0x5F3759DF - (1 << 22))
POOL_ROUNDS = (1, 2, 3)
DVE_ROUNDS = tuple(r for r in range(RND) if r not in POOL_ROUNDS)
NEWTON = 3
SCALE = float(HD) ** -0.5

FFN_PIECES = [
    [("D", 0, 0), ("D", 0, 1), ("D", 1, 0), ("D", 1, 1), ("D", 2, 0), ("D", 2, 1)],
    [("D", 3, 0), ("D", 3, 1), ("G", 0), ("U", 0), ("G", 1), ("U", 1)],
    [("G", 2), ("U", 2), ("G", 3), ("U", 3), ("G", 4), ("U", 4)],
    [("G", 5), ("U", 5), ("G", 6), ("U", 6), ("G", 7), ("U", 7)],
]


class Step:

    def __init__(self, turn, half, q, looped):
        self.turn, self.half, self.q, self.looped = turn, half, q, looped
        self.grp = turn * 2 + half

    def back(self, n):
        place = GROUP * self.half + self.q - n
        turns, place = divmod(place, 2 * GROUP)
        return Step(self.turn + turns if turns else self.turn, place // GROUP, place % GROUP, self.looped)

    def exists(self):
        return self.looped or 0 <= GROUP * self.grp + self.q < PAIRS

    def done(self, back=0, per=1):
        return self.grp * (GROUP * per) + per * (self.q - back + 1)

    def part(self, n, per=RND):
        return self.grp * (GROUP * per) + (per * self.q + n)

    def group_count(self, per_group, back, extra=0):
        return self.grp * per_group + (extra - per_group * back)

    def ring(self, n):
        return (GROUP * self.half + self.q) % n

    def pieces(self):
        out = []
        for piece in FFN_PIECES[self.q]:
            back = 2 if piece[0] == "D" else 1
            ok = self.looped or 0 <= self.grp - back < GROUPS
            out.append(piece if ok else None)
        return out


def slots(eng, emit):
    two_groups = [(half, q) for half in range(2) for q in range(GROUP)]
    for half, q in two_groups:
        emit(Step(0, half, q, False))
    with eng.Fori(1, GROUPS // 2) as turn:
        for half, q in two_groups:
            emit(Step(turn, half, q, True))
    for half, q in two_groups[:GROUP + 4]:
        emit(Step(GROUPS // 2, half, q, False))


def run(work, pair, *more):
    if pair.exists():
        work(pair, *more)


def head_pair(r, tt):
    return 2 * (TPR * (r // 2) + tt) + r % 2


def wait(eng, sem, value):
    if not isinstance(value, int) or value > 0:
        eng.wait_ge(sem, value)


def flamingo_block(nc, x, ctx_in, g_attn, g_ffn, w_qkv, w_up, w_down, out):
    x_t = x.rearrange("(i t b) s d -> i t (b s) d", b=P // SEQ, t=2 * GROUP)
    c_t = ctx_in.rearrange("(i t b) s d -> i t (b s) d", b=P // SEQ, t=2 * GROUP)
    out_g = out.rearrange("(i g t b) s d -> i g (b s) t d", b=P // SEQ, t=GROUP, g=2)
    wqkv_d = w_qkv.rearrange("(k p) n -> p k n", p=P)
    wup_d = w_up.rearrange("(k p) n -> p k n", p=P)
    wdn_d = w_down.rearrange("(k p) n -> p k n", p=P)

    stack = ExitStack()
    with stack:
        def sb(name, shape, dt=F32):
            return stack.enter_context(nc.sbuf_tensor(name, shape, dt))

        def sem(name):
            return stack.enter_context(nc.semaphore(name))

        wqkv_hi, wqkv_lo = (sb(f"wqkv_{n}", [P, KD, 3 * DIM], F32R) for n in ("hi", "lo"))
        wup_hi, wup_lo = (sb(f"wup_{n}", [P, KD, 2 * HIDDEN], F32R) for n in ("hi", "lo"))
        wdn_hi, wdn_lo = (sb(f"wdn_{n}", [P, CH, DIM], F32R) for n in ("hi", "lo"))
        stage = sb("stage", [P, 2, 1024])
        ident32 = sb("ident32", [P, P])
        ident16 = sb("ident16", [P, P], F16)
        neg_half = sb("neg_half", [P, 1])
        one_and_half = sb("one_and_half", [P, 1])
        eps = sb("eps", [P, 1])
        gates = sb("gates", [P, 2])
        tgates = sb("tgates", [P, 2])
        ffn_gate = sb("ffn_gate", [P, 1])

        xbuf = sb("xbuf", [P, 4, DIM])
        cbuf = sb("cbuf", [P, 4, DIM])
        st1, mv1, ve1, rstd1 = sb("st1", [P, 6]), sb("mv1", [P, 2]), sb("ve1", [P, 1]), sb("rstd1", [P, 1])
        st2, mv2, ve2, rstd2 = sb("st2", [P, 6]), sb("mv2", [P, 2]), sb("ve2", [P, 1]), sb("rstd2", [P, 1])
        spare = sb("spare", [P, 2])
        xn = sb("xn", [P, 2, DIM])
        tT_hi, tT_lo = (sb(f"tT_{n}", [P, 2 * KD, P], F32R) for n in ("hi", "lo"))
        sq = sb("sq", [P, 2 * DIM])
        ss, half_ms, rqk, nt = (sb(n, [P, 2 * HEADS]) for n in ("ss", "half_ms", "rqk", "nt"))
        qk32 = sb("qk32", [P, 2 * DIM])
        q4 = sb("q4", [P, HEADS, 4, HD], F16)
        k4 = sb("k4", [P, HEADS, 4, HD], F16)
        qT = sb("qT", [P, GRP_T, 2, SEQ], F16)
        kT = sb("kT", [P, GRP_T, 2, 2, SEQ], F16)
        parity = sb("parity", [P, 2])
        vrem = sb("vrem", [P, DIM])
        vn = sb("vn", [P, HEADS, 3, HD], BF16)
        vp_flat = sb("vp", [P, 4 * HEADS * VW], BF16)
        vp = vp_flat[:, :].rearrange("p (u t b a c) -> p u t b a c", u=2, b=2, a=2, c=VW)
        p32 = sb("p32", [P, RND, 512])
        p_hi = sb("p_hi", [P, RND, 512], F16)
        p_lo = sb("p_lo", [P, RND, 512], F16)
        oa = sb("oa", [P, HEADS, VW])
        asum = sb("asum", [P, DIM])
        rinv = sb("rinv", [P, HEADS])
        xr = sb("xr", [P, 8, DIM])
        yn = sb("yn", [P, 2, DIM])
        yT_hi, yT_lo = (sb(f"yT_{n}", [P, 2, KD, 512], F32R) for n in ("hi", "lo"))
        hb = sb("hb", [P, 3, 512])
        h_hi, h_lo = (sb(f"h_{n}", [P, CH, 512], F32R) for n in ("hi", "lo"))
        obuf = sb("obuf", [P, GROUP, DIM])

        bank = [stack.enter_context(nc.psum_tensor(f"bank{i}", [P, 512], F32)) for i in range(8)]
        ffn_ps = bank[0:3]
        tr_ps, qk_ps, o_ps = bank[3:6]
        s_ps = bank[6:8]
        v_ps = tr_ps[:, 0:DIM]
        y_ps = tr_ps[:, DIM:2 * DIM]
        qT_ps, kT_ps = (b[:, :].bitcast(F16) for b in s_ps)

        def ffn_bank(piece):
            kind, n = piece[0], piece[1]
            return ffn_ps[(n if kind == "D" else GROUP + 2 * n + (kind == "U")) % 3]

        names = """x_in0 x_in1 x_in2 x_in3 c_in0 c_in1 c_in2 c_in3 w_in0 w_in1 gate_in out_stored
            zeroed parity_made ident_made const_made w_hi w_lo tanh_g gate_half
            bn1 mv1_done ve1_done rstd1_done xn_done tr_done tT_hi_done tT_lo_done qk_done v_done
            sq_done ss_done half_ms_done seeded newton nt1 nt2 nt3 norm_done hi_q hi_k lo_q lo_k
            qT_tr kT_tr qT_done kT_done
            v1_done vrem_done v2_done v3_done vp_done s_done p32_done p_hi_done p_lo_done p_lo_pool pv_done
            o_done asum_done rinv_done attn_done x1_done bn2 mv2_done ve2_done rstd2_done yn_done
            y_tr yT_hi_done yT_lo_done up_done tanh_done gt_done h_done h_hi_done h_lo_done
            down_done out_ready""".split()
        S = {n: sem(n) for n in names}
        x_in = [S[f"x_in{i}"] for i in range(4)]
        c_in = [S[f"c_in{i}"] for i in range(4)]
        w_in = [S[f"w_in{i}"] for i in range(2)]

        pieces = [(wqkv_d[:, k, :], wqkv_hi[:, k, :], wqkv_lo[:, k, :]) for k in range(KD)]
        for k in range(KD):
            for u in range(2):
                c = slice(u * HIDDEN, (u + 1) * HIDDEN)
                pieces.append((wup_d[:, k, c], wup_hi[:, k, c], wup_lo[:, k, c]))
        for u in range(2):
            c = slice(4 * u, 4 * u + 4)
            flat = "p k n -> p (k n)"
            pieces.append((wdn_d[:, c, :], wdn_hi[:, c, :].rearrange(flat), wdn_lo[:, c, :].rearrange(flat)))
        QKV_PIECES, UP_PIECES = KD, 3 * KD

        def staged(i):
            return stage[:, i % 2, 0:pieces[i][1].shape[1]]

        def split_in_slot(s):
            if s.looped or s.grp > 0 or not 1 <= s.q <= 3:
                return []
            return [QKV_PIECES + 2 * s.q - 2, QKV_PIECES + 2 * s.q - 1]

        block = stack.enter_context(nc.Block())

        @block.sync
        def _(sp):
            def load_weights(i):
                if i >= 2:
                    sp.wait_ge(S["w_lo"], i - 1)
                dst = staged(i)
                if i >= UP_PIECES:
                    dst = dst.rearrange("p (k n) -> p k n", n=DIM)
                sp.dma_start(dst, pieces[i][0]).then_inc(w_in[i % 2], 16)

            def load_pair(s):
                pair = GROUP * s.half + s.q
                wait(sp, S["x1_done"], s.done(4))
                sp.dma_start(xbuf[:, s.q, :], x_t[s.turn, pair, :, :]).then_inc(x_in[s.q], 16)
                sp.dma_start(cbuf[:, s.q, :], c_t[s.turn, pair, :, :]).then_inc(c_in[s.q], 16)

            load_pair(Step(0, 0, 0, False))
            load_weights(0)
            load_weights(1)
            for q in range(1, GROUP):
                load_pair(Step(0, 0, q, False))
            for col, g in enumerate((g_attn, g_ffn)):
                sp.dma_start(gates[:, col:col + 1], g.partition_broadcast(P)).then_inc(S["gate_in"], 16)
            for i in range(2, len(pieces)):
                load_weights(i)
            for q in range(GROUP):
                load_pair(Step(0, 1, q, False))
            with sp.Fori(1, GROUPS // 2) as turn:
                for half in range(2):
                    for q in range(GROUP):
                        load_pair(Step(turn, half, q, True))

        @block.tensor
        def _(pe):
            mm = nc.tensor.matmul

            def product(o, left, right, first, last):
                (lh, ll), (rh, rl) = left, right
                mm(o, lh, rh, start=first, stop=False)
                mm(o, lh, rl, start=False, stop=False)
                return mm(o, ll, rh, start=False, stop=last)

            def transposes(s):
                pe.wait_ge(c_in[s.q], s.group_count(16, -1))
                wait(pe, S["vrem_done"], s.done(1))
                wait(pe, S["yT_lo_done"], s.done(4))
                pe.wait_ge(S["xn_done"], s.done())
                for k in range(KD):
                    nc.tensor.transpose(tr_ps[:, k * P:(k + 1) * P], xn[:, s.ring(2), k * P:(k + 1) * P],
                                        ident32[:, :])
                for k in range(KD):
                    last = nc.tensor.transpose(tr_ps[:, (KD + k) * P:(KD + k + 1) * P],
                                               cbuf[:, s.q, k * P:(k + 1) * P], ident32[:, :])
                last.then_inc(S["tr_done"], 1)

            def project(s):
                if not s.looped:
                    pe.wait_ge(S["w_lo"], QKV_PIECES)
                pe.wait_ge(S["tT_hi_done"], s.done())
                pe.wait_ge(S["tT_lo_done"], s.done())

                def one(o, part, col):
                    for k in range(KD):
                        last = product(o, (tT_hi[:, KD * part + k, :], tT_lo[:, KD * part + k, :]),
                                       (wqkv_hi[:, k, col:col + DIM], wqkv_lo[:, k, col:col + DIM]),
                                       k == 0, k == KD - 1)
                    return last

                one(v_ps, 1, 2 * DIM).then_inc(S["v_done"], 1)
                wait(pe, S["norm_done"], s.done(1))
                one(qk_ps[:, 0:DIM], 0, 0)
                one(qk_ps[:, DIM:2 * DIM], 1, DIM).then_inc(S["qk_done"], 1)

            def qk_transposes(s):
                pe.wait_ge(S["lo_q"], s.done())
                pe.wait_ge(S["lo_k"], s.done())
                wait(pe, S["p_hi_done"], s.done(1, RND))
                q_rows = q4[:, :, :, :].rearrange("p (g h) c d -> p g (h c d)", g=GRP_T)
                k_rows = k4[:, :, :, :].rearrange("p (g h) c d -> p g (h c d)", g=GRP_T)
                for rows, ps, done in ((q_rows, qT_ps, "qT_tr"), (k_rows, kT_ps, "kT_tr")):
                    for g in range(GRP_T):
                        last = nc.tensor.transpose(ps[:, g * P:(g + 1) * P], rows[:, g, :], ident16[:, :])
                    last.then_inc(S[done], 1)

            def scores(s, r):
                if r == 0:
                    pe.wait_ge(S["qT_done"], s.done())
                    pe.wait_ge(S["kT_done"], s.done())
                if r >= 2:
                    pe.wait_ge(S["p_hi_done"], s.part(r - 1))
                o = s_ps[r % 2][:, :].rearrange("p (t b n) -> p t b n", t=TPR, b=2)
                rows = slice(SEQ * (r % 2), SEQ * (r % 2) + SEQ)
                for tt in range(TPR):
                    g = TPR * (r // 2) + tt
                    for b in range(2):
                        keys = kT[rows, g, b, :, :].rearrange("p a m -> p (a m)")
                        last = mm(o[:, tt, b, :], keys, qT[rows, g, b, :], start=True, stop=True)
                last.then_inc(S["s_done"], 1)

            def attend(s, r):
                if r == 0:
                    pe.wait_ge(S["vp_done"], s.done())
                wait(pe, S["o_done"], s.part(r))
                if r in POOL_ROUNDS:
                    pe.wait_ge(S["p_lo_pool"], s.part(POOL_ROUNDS.index(r) + 1, len(POOL_ROUNDS)))
                else:
                    pe.wait_ge(S["p_lo_done"], s.part(DVE_ROUNDS.index(r) + 1, len(DVE_ROUNDS)))
                o = o_ps[:, 0:TPR * 4 * VW].rearrange("p (t c) -> p t c", t=TPR)
                for tt in range(TPR):
                    values = vp[:, s.ring(2), head_pair(r, tt), :, :, :].rearrange("p b a c -> p (b a) c")
                    cols = slice(tt * P, (tt + 1) * P)
                    mm(o[:, tt, :], p_hi[:, r, cols], values.rearrange("p a c -> p (a c)"), start=True, stop=False)
                    last = mm(o[:, tt, :].rearrange("p (a c) -> p a c", c=VW)[:, :, HD:VW],
                              p_lo[:, r, cols], values[:, :, HD:VW], start=False, stop=True)
                last.then_inc(S["pv_done"], 1)

            def y_transposes(s):
                pe.wait_ge(S["yn_done"], s.done())
                pe.wait_ge(S["vrem_done"], s.done(-3) if s.back(-3).exists() else PAIRS)
                for k in range(KD):
                    last = nc.tensor.transpose(y_ps[:, k * P:(k + 1) * P], yn[:, s.ring(2), k * P:(k + 1) * P],
                                               ident32[:, :])
                last.then_inc(S["y_tr"], 1)

            def ffn_piece(s, i):
                piece = s.pieces()[i]
                if piece is None:
                    return
                if piece[0] == "D":
                    _, j, part = piece
                    if (j, part) == (0, 0):
                        pe.wait_ge(S["h_hi_done"], s.group_count(CH, 1))
                        pe.wait_ge(S["h_lo_done"], s.group_count(CH, 1))
                        if not s.looped:
                            pe.wait_ge(S["w_lo"], len(pieces))
                    if j >= 3 and part == 0:
                        pe.wait_ge(S["out_ready"], s.group_count(GROUP, 2, j - 2))
                    o = ffn_bank(piece)[:, 0:DIM]
                    tok = slice(j * P, (j + 1) * P)
                    for c in range(CH // 2 * part, CH // 2 * (part + 1)):
                        last = product(o, (h_hi[:, c, tok], h_lo[:, c, tok]), (wdn_hi[:, c, :], wdn_lo[:, c, :]),
                                       c == 0, c == CH - 1)
                    if part:
                        last.then_inc(S["down_done"], 1)
                    return
                up, c = piece[0] == "U", piece[1]
                if c == 0 and not up:
                    pe.wait_ge(S["yT_hi_done"], s.group_count(GROUP, 0))
                    pe.wait_ge(S["yT_lo_done"], s.group_count(GROUP, 0))
                    if not s.looped:
                        pe.wait_ge(S["w_lo"], UP_PIECES)
                n = 2 * c + up
                if n < 3:
                    wait(pe, S["out_ready"], s.group_count(GROUP, 2, n + 2) if s.looped or s.grp > 1 else 0)
                elif up:
                    pe.wait_ge(S["gt_done"], s.group_count(CH, 1, c))
                else:
                    pe.wait_ge(S["h_done"], s.group_count(CH, 1, c - 1))
                col = slice(up * HIDDEN + c * P, up * HIDDEN + (c + 1) * P)
                half = 1 - s.half
                for k in range(KD):
                    last = product(ffn_bank(piece)[:, :], (wup_hi[:, k, col], wup_lo[:, k, col]),
                                   (yT_hi[:, half, k, :], yT_lo[:, half, k, :]), k == 0, k == KD - 1)
                last.then_inc(S["up_done"], 1)

            pe.wait_ge(S["ident_made"], 2)
            pe.wait_ge(S["zeroed"], 2)

            def emit(s):
                run(attend, s.back(3), 1)
                run(qk_transposes, s.back(2))
                run(attend, s.back(3), 2)
                run(project, s.back(1))
                ffn_piece(s.back(2), 0)
                run(scores, s.back(2), 0)
                run(y_transposes, s.back(4))
                ffn_piece(s.back(2), 1)
                run(attend, s.back(3), 3)
                run(scores, s.back(2), 1)
                run(transposes, s)
                ffn_piece(s.back(2), 2)
                run(scores, s.back(2), 2)
                run(attend, s.back(2), 0)
                ffn_piece(s.back(2), 3)
                ffn_piece(s.back(2), 4)
                run(scores, s.back(2), 3)
                ffn_piece(s.back(2), 5)

            slots(pe, emit)

        @block.scalar
        def _(act):
            def split_weights(i):
                act.wait_ge(w_in[i % 2], 16 * (i // 2 + 1))
                nc.scalar.activation(pieces[i][1], staged(i), ACT.Copy).then_inc(S["w_hi"], 1)

            def split_more(s):
                for i in split_in_slot(s):
                    split_weights(i)

            def exps(s, r):
                act.wait_ge(S["s_done"], s.part(r + 1))
                nc.scalar.activation(p32[:, r, :], s_ps[r % 2][:, :], ACT.Exp, scale=SCALE).then_inc(S["p32_done"], 1)
                nc.scalar.activation(p_hi[:, r, :], s_ps[r % 2][:, :], ACT.Exp, scale=SCALE).then_inc(S["p_hi_done"], 1)

            def t_hi(s):
                act.wait_ge(S["tr_done"], s.done())
                nc.scalar.activation(tT_hi[:, :, :].rearrange("p k n -> p (k n)"), tr_ps[:, :],
                                     ACT.Copy).then_inc(S["tT_hi_done"], 1)

            def v_first(s):
                act.wait_ge(S["v_done"], s.done())
                wait(act, S["vp_done"], s.done(1))
                nc.scalar.activation(vn[:, :, 1, :], v_ps.rearrange("p (h d) -> p h d", d=HD),
                                     ACT.Copy).then_inc(S["v1_done"], 1)

            def squares(s):
                act.wait_ge(S["qk_done"], s.done())
                nc.scalar.activation(sq[:, :], qk_ps[:, :], ACT.Square, scale=float(HD) ** -0.5).then_inc(S["sq_done"], 1)

            def v_second(s):
                act.wait_ge(S["vrem_done"], s.done())
                nc.scalar.activation(vn[:, :, 2, :], vrem[:, :].rearrange("p (h d) -> p h d", d=HD),
                                     ACT.Copy).then_inc(S["v2_done"], 1)

            def y_hi(s):
                act.wait_ge(S["y_tr"], s.done())
                nc.scalar.activation(yT_hi[:, s.half, :, s.q * P:(s.q + 1) * P],
                                     y_ps.rearrange("p (k n) -> p k n", k=KD),
                                     ACT.Copy).then_inc(S["yT_hi_done"], 1)

            def k_high(s):
                act.wait_ge(S["norm_done"], s.done())
                k = qk32[:, DIM:2 * DIM].rearrange("p (h d) -> p h d", d=HD)
                nc.scalar.activation(k4[:, :, 0:4:2, :], k.unsqueeze(2).broadcast_to([P, HEADS, 2, HD]),
                                     ACT.Copy).then_inc(S["hi_k"], 1)

            def take_k(s):
                act.wait_ge(S["kT_tr"], s.done())
                for a in range(2):
                    last = nc.scalar.activation(kT[:, :, :, a, :], kT_ps[:, :].rearrange("p (g b m) -> p g b m", b=2, m=SEQ),
                                                ACT.Copy, scale=parity[:, a:a + 1])
                last.then_inc(S["kT_done"], 1)

            def take_o(s, r):
                act.wait_ge(S["pv_done"], s.part(r + 1))
                if r == 0:
                    wait(act, S["rinv_done"], s.done(1))
                    wait(act, S["asum_done"], s.done(1))
                for b in range(2):
                    rows = slice(SEQ * b, SEQ * (b + 1))
                    o = o_ps[rows, 0:TPR * 4 * VW].rearrange("p (t b c) -> p t b c", t=TPR, b=2)
                    to = oa[rows, :, :].rearrange("p (g u a) c -> p g u (a c)", u=2, a=2)
                    g = TPR * (r // 2)
                    last = nc.scalar.activation(to[:, g:g + TPR, r % 2, :], o[:, :, b, :], ACT.Copy)
                last.then_inc(S["o_done"], 1)

            def ffn_event(s, i):
                piece = s.pieces()[i]
                if piece is None or piece[0] == "D":
                    return
                c = piece[1]
                if piece[0] == "G":
                    act.wait_ge(S["up_done"], s.group_count(2 * CH, 1, 2 * c + 1))
                    wait(act, S["h_lo_done"], s.group_count(CH, 1, max(c - 2, 0)))
                    nc.scalar.activation(hb[:, c % 3, :], ffn_bank(piece)[:, :], ACT.Tanh,
                                         scale=0.5).then_inc(S["tanh_done"], 1)
                else:
                    act.wait_ge(S["h_done"], s.group_count(CH, 1, c + 1))
                    nc.scalar.activation(h_hi[:, c, :], hb[:, c % 3, :], ACT.Copy).then_inc(S["h_hi_done"], 1)

            def store_out(s):
                if s.looped or s.grp >= 2:
                    if s.q == 1:
                        act.wait_ge(S["out_ready"], s.group_count(GROUP, 1))
                        act.dma_start(out_g[s.turn - 1, s.half, :, :, :], obuf[:, :, :]).then_inc(S["out_stored"], 16)
                    elif s.q == 2:
                        act.wait_ge(S["out_stored"], s.group_count(16, 1))

            for i in range(QKV_PIECES):
                split_weights(i)
            act.wait_ge(S["gate_in"], 32)
            nc.scalar.activation(tgates[:, :], gates[:, :], ACT.Tanh).then_inc(S["tanh_g"], 1)

            def emit(s):
                run(take_k, s.back(2))
                run(v_first, s.back(1))
                run(squares, s.back(1))
                run(v_second, s.back(1))
                run(take_o, s.back(3), 2)
                ffn_event(s.back(2), 0)
                run(y_hi, s.back(4))
                run(exps, s.back(2), 0)
                run(take_o, s.back(3), 3)
                ffn_event(s.back(2), 1)
                run(t_hi, s)
                run(exps, s.back(2), 1)
                ffn_event(s.back(2), 2)
                store_out(s.back(2))
                run(exps, s.back(2), 2)
                run(take_o, s.back(2), 0)
                run(k_high, s.back(1))
                ffn_event(s.back(2), 4)
                ffn_event(s.back(2), 3)
                run(exps, s.back(2), 3)
                run(take_o, s.back(2), 1)
                split_more(s)
                ffn_event(s.back(2), 5)

            act.wait_ge(S["parity_made"], 2)
            slots(act, emit)
            act.wait_ge(S["out_stored"], 16 * GROUPS)

        @block.vector
        def _(dve):
            v = nc.vector
            v.memset(parity[:, :], 0.0).then_inc(S["parity_made"], 1)
            dve.wait_ge(S["parity_made"], 1)
            for j in range(4):
                last = v.memset(parity[32 * j:32 * j + 32, j % 2:j % 2 + 1], 1.0)
            last.then_inc(S["parity_made"], 1)
            v.memset(one_and_half[:, :], 1.5)
            v.memset(neg_half[:, :], -0.5).then_inc(S["const_made"], 1)
            v.memset(vp_flat[:, :].bitcast(F32), 0.0).then_inc(S["zeroed"], 1)
            dve.wait_ge(S["zeroed"], 1)
            for a in range(2):
                last = v.memset(vp[SEQ * a:SEQ * (a + 1), :, :, :, a, 3 * HD:VW], 1.0)
            last.then_inc(S["zeroed"], 1)

            def split_weights(i):
                dve.wait_ge(S["w_hi"], i + 1)
                v.tensor_tensor(pieces[i][2], staged(i), pieces[i][1].bitcast(F32), ALU.subtract).then_inc(S["w_lo"], 1)

            def split_more(s):
                for i in split_in_slot(s):
                    split_weights(i)

            def first_stats(s):
                dve.wait_ge(x_in[s.q], s.group_count(16, -1))
                v.bn_stats(st1[:, :], xbuf[:, s.q, :]).then_inc(S["bn1"], 1)

            def first_mean(s):
                dve.wait_ge(S["bn1"], s.done())
                v.memset(spare[:, 0:1], 0.0)
                v.bn_aggr(mv1[:, :], st1[:, :]).then_inc(S["mv1_done"], 1)

            def first_norm(s):
                dve.wait_ge(S["rstd1_done"], s.done())
                v.tensor_scalar(xn[:, s.ring(2), :], xbuf[:, s.q, :], mv1[:, 0:1], rstd1[:, 0:1],
                                ALU.subtract, ALU.mult).then_inc(S["xn_done"], 1)

            def t_lo(s):
                dve.wait_ge(S["tT_hi_done"], s.done())
                flat = "p k n -> p (k n)"
                v.tensor_tensor(tT_lo[:, :, :].rearrange(flat), tr_ps[:, :],
                                tT_hi[:, :, :].rearrange(flat).bitcast(F32), ALU.subtract).then_inc(S["tT_lo_done"], 1)

            def v_rest(s):
                dve.wait_ge(S["v1_done"], s.done())
                v.tensor_tensor(vrem[:, :].rearrange("p (h d) -> p h d", d=HD),
                                v_ps.rearrange("p (h d) -> p h d", d=HD), vn[:, :, 1, :],
                                ALU.subtract).then_inc(S["vrem_done"], 1)

            def sums_of_squares(s):
                dve.wait_ge(S["sq_done"], s.done())
                v.tensor_reduce(ss[:, :], sq[:, :].rearrange("p (h d) -> p h d", d=HD), AX.X, ALU.add).then_inc(S["ss_done"], 1)

            def half_means(s):
                dve.wait_ge(S["ss_done"], s.done())
                v.tensor_scalar(half_ms[:, :], ss[:, :], RMS_EPS, 0.5, ALU.add, ALU.mult).then_inc(S["half_ms_done"], 1)

            def guess(s):
                dve.wait_ge(S["half_ms_done"], s.done())
                v.tensor_scalar(rqk[:, :].bitcast(I32), half_ms[:, :].bitcast(I32), -0.5, RSQRT_BITS,
                                ALU.mult, ALU.add).then_inc(S["seeded"], 1)

            def qk_norm(s):
                dve.wait_ge(S["newton"], s.done(0, NEWTON))
                v.tensor_tensor(qk32[:, :].rearrange("p (h d) -> p h d", d=HD),
                                qk_ps[:, :].rearrange("p (h d) -> p h d", d=HD),
                                rqk[:, :].unsqueeze(2).broadcast_to([P, 2 * HEADS, HD]), ALU.mult).then_inc(S["norm_done"], 1)

            def doubled(w):
                qk = qk32[:, :].rearrange("p (w h d) -> p w h d", w=2, d=HD)
                return qk[:, w, :, :].unsqueeze(2).broadcast_to([P, HEADS, 2, HD])

            def q_high(s):
                dve.wait_ge(S["norm_done"], s.done())
                v.tensor_copy(q4[:, :, 0:2, :], doubled(0)).then_inc(S["hi_q"], 1)

            def q_low(s):
                dve.wait_ge(S["hi_q"], s.done())
                v.tensor_tensor(q4[:, :, 2:4, :], doubled(0), q4[:, :, 0:2, :], ALU.subtract).then_inc(S["lo_q"], 1)

            def k_low(s):
                dve.wait_ge(S["hi_k"], s.done())
                v.tensor_tensor(k4[:, :, 1:4:2, :], doubled(1), k4[:, :, 0:4:2, :], ALU.subtract).then_inc(S["lo_k"], 1)

            def lay_out_values(s):
                dve.wait_ge(S["v3_done"], s.done())
                wait(dve, S["pv_done"], s.done(2, RND))
                for a in range(2):
                    for b in range(2):
                        src = vn[SEQ * b:SEQ * (b + 1), :, :, :].rearrange("p (t a) c d -> p t a (c d)", a=2)
                        last = v.tensor_copy(vp[SEQ * a:SEQ * (a + 1), s.ring(2), :, b, a, 0:3 * HD], src[:, :, a, :])
                last.then_inc(S["vp_done"], 1)

            def p_rest(s, r):
                dve.wait_ge(S["p_hi_done"], s.part(r + 1))
                v.tensor_tensor(p_lo[:, r, :], p32[:, r, :], p_hi[:, r, :], ALU.subtract).then_inc(S["p_lo_done"], 1)

            def attention_sums(s):
                dve.wait_ge(S["o_done"], s.done(0, RND))
                parts = oa[:, :, 0:3 * HD].rearrange("p h (c d) -> p h d c", d=HD)
                v.tensor_reduce(asum[:, :].rearrange("p (h d) -> p h d", d=HD), parts, AX.X, ALU.add).then_inc(S["asum_done"], 1)

            def inverses(s):
                dve.wait_ge(S["o_done"], s.done(0, RND))
                v.reciprocal(rinv[:, :], oa[:, :, 3 * HD]).then_inc(S["rinv_done"], 1)

            def normalize(s):
                dve.wait_ge(S["asum_done"], s.done())
                dve.wait_ge(S["rinv_done"], s.done())
                a3 = asum[:, :].rearrange("p (h d) -> p h d", d=HD)
                v.tensor_tensor(a3, a3, rinv[:, :].unsqueeze(2).broadcast_to([P, HEADS, HD]), ALU.mult).then_inc(S["attn_done"], 1)

            def residual(s):
                dve.wait_ge(S["attn_done"], s.done())
                v.scalar_tensor_tensor(out=xr[:, s.ring(8), :], in0=asum[:, :], scalar=tgates[:, 0:1], in1=xbuf[:, s.q, :],
                                       op0=ALU.mult, op1=ALU.add).then_inc(S["x1_done"], 1)

            def second_stats(s):
                dve.wait_ge(S["x1_done"], s.done())
                v.bn_stats(st2[:, :], xr[:, s.ring(8), :]).then_inc(S["bn2"], 1)

            def second_mean(s):
                dve.wait_ge(S["bn2"], s.done())
                v.memset(spare[:, 1:2], 0.0)
                v.bn_aggr(mv2[:, :], st2[:, :]).then_inc(S["mv2_done"], 1)

            def second_norm(s):
                dve.wait_ge(S["rstd2_done"], s.done())
                v.tensor_scalar(yn[:, s.ring(2), :], xr[:, s.ring(8), :], mv2[:, 0:1], rstd2[:, 0:1],
                                ALU.subtract, ALU.mult).then_inc(S["yn_done"], 1)

            def y_lo(s):
                dve.wait_ge(S["yT_hi_done"], s.done())
                cols = slice(s.q * P, (s.q + 1) * P)
                v.tensor_tensor(yT_lo[:, s.half, :, cols], y_ps.rearrange("p (k n) -> p k n", k=KD),
                                yT_hi[:, s.half, :, cols].bitcast(F32), ALU.subtract).then_inc(S["yT_lo_done"], 1)

            def ffn_event(s, i):
                piece = s.pieces()[i]
                if piece is None:
                    return
                if piece[0] == "D":
                    _, j, part = piece
                    if part:
                        dve.wait_ge(S["down_done"], s.group_count(GROUP, 2, j + 1))
                        pair = GROUP * s.half + j
                        v.scalar_tensor_tensor(out=obuf[:, j, :], in0=ffn_bank(piece)[:, 0:DIM], scalar=ffn_gate[:, 0:1],
                                               in1=xr[:, pair, :], op0=ALU.mult, op1=ALU.add).then_inc(S["out_ready"], 1)
                    return
                c = piece[1]
                buf = hb[:, c % 3, :]
                if piece[0] == "G":
                    dve.wait_ge(S["tanh_done"], s.group_count(CH, 1, c + 1))
                    v.scalar_tensor_tensor(out=buf, in0=buf, scalar=1.0, in1=ffn_bank(piece)[:, :],
                                           op0=ALU.add, op1=ALU.mult).then_inc(S["gt_done"], 1)
                else:
                    dve.wait_ge(S["up_done"], s.group_count(2 * CH, 1, 2 * c + 2))
                    dve.wait_ge(S["gt_done"], s.group_count(CH, 1, c + 1))
                    v.tensor_tensor(buf, buf, ffn_bank(piece)[:, :], ALU.mult).then_inc(S["h_done"], 1)

            for i in range(QKV_PIECES):
                split_weights(i)
            dve.wait_ge(S["tanh_g"], 1)
            v.tensor_scalar(ffn_gate[:, :], tgates[:, 1:2], 0.5, None, ALU.mult).then_inc(S["gate_half"], 1)
            dve.wait_ge(S["gate_half"], 1)

            def take_q(s):
                dve.wait_ge(S["qT_tr"], s.done())
                v.tensor_copy(qT[:, :, :, :].rearrange("p g b n -> p (g b n)"), qT_ps[:, :]).then_inc(S["qT_done"], 1)

            def emit(s):
                run(first_stats, s)
                run(take_q, s.back(2))
                run(first_mean, s)
                run(second_norm, s.back(4))
                run(v_rest, s.back(1))
                run(sums_of_squares, s.back(1))
                run(half_means, s.back(1))
                run(guess, s.back(1))
                run(first_norm, s)
                ffn_event(s.back(2), 0)
                run(y_lo, s.back(4))
                ffn_event(s.back(2), 1)
                run(p_rest, s.back(2), 0)
                run(inverses, s.back(3))
                run(attention_sums, s.back(3))
                run(lay_out_values, s.back(1))
                run(normalize, s.back(3))
                ffn_event(s.back(2), 2)
                run(residual, s.back(3))
                run(qk_norm, s.back(1))
                ffn_event(s.back(2), 3)
                run(q_high, s.back(1))
                run(k_low, s.back(1))
                ffn_event(s.back(2), 4)
                run(q_low, s.back(1))
                ffn_event(s.back(2), 5)
                run(t_lo, s)
                run(second_stats, s.back(3))
                run(second_mean, s.back(3))
                split_more(s)

            slots(dve, emit)

        @block.gpsimd
        def _(pool):
            g = nc.gpsimd
            g.memset(eps[:, :], LN_EPS)
            g.memset(ident32[:, :], 0.0).then_inc(S["const_made"], 1)
            g.memset(ident16[:, :], 0.0).then_inc(S["const_made"], 1)
            pool.wait_ge(S["const_made"], 3)
            for ident in (ident32, ident16):
                g.affine_select(out=ident[:, :], in_=ident[:, :], compare_op=ALU.not_equal, fill=1.0, base=0,
                                pattern=[[-1, P]], channel_multiplier=1).then_inc(S["ident_made"], 1)

            def variance(s, mv, ve, n):
                pool.wait_ge(S["mv" + n + "_done"], s.done())
                g.tensor_tensor(ve[:, :], mv[:, 1:2], eps[:, 0:1], ALU.add).then_inc(S["ve" + n + "_done"], 1)

            def rstd(s, ve, r, n):
                pool.wait_ge(S["ve" + n + "_done"], s.done())
                g.tensor_tensor(r[:, :], ve[:, :], neg_half[:, 0:1], ALU.pow).then_inc(S["rstd" + n + "_done"], 1)

            def newton(s, n):
                if n == 0:
                    pool.wait_ge(S["seeded"], s.done())
                else:
                    pool.wait_ge(S["newton"], s.part(n, NEWTON))
                g.tensor_tensor(nt[:, :], half_ms[:, :], rqk[:, :], ALU.mult).then_inc(S["nt1"], 1)
                pool.wait_ge(S["nt1"], s.part(n + 1, NEWTON))
                g.tensor_tensor(nt[:, :], nt[:, :], rqk[:, :], ALU.mult).then_inc(S["nt2"], 1)
                pool.wait_ge(S["nt2"], s.part(n + 1, NEWTON))
                g.tensor_tensor(nt[:, :], one_and_half[:, 0:1].broadcast_to([P, 2 * HEADS]), nt[:, :],
                                ALU.subtract).then_inc(S["nt3"], 1)
                pool.wait_ge(S["nt3"], s.part(n + 1, NEWTON))
                g.tensor_tensor(rqk[:, :], rqk[:, :], nt[:, :], ALU.mult).then_inc(S["newton"], 1)

            def v_third(s):
                pool.wait_ge(S["v2_done"], s.done())
                g.tensor_tensor(vn[:, :, 0, :], vrem[:, :].rearrange("p (h d) -> p h d", d=HD), vn[:, :, 2, :],
                                ALU.subtract).then_inc(S["v3_done"], 1)

            def h_rest(s, i):
                piece = s.pieces()[i]
                if piece is None or piece[0] != "U":
                    return
                c = piece[1]
                pool.wait_ge(S["h_hi_done"], s.group_count(CH, 1, c + 1))
                g.tensor_tensor(h_lo[:, c, :], hb[:, c % 3, :], h_hi[:, c, :].bitcast(F32), ALU.subtract).then_inc(S["h_lo_done"], 1)

            def p_rest(s, r):
                pool.wait_ge(S["p_hi_done"], s.part(r + 1))
                g.tensor_tensor(p_lo[:, r, :], p32[:, r, :], p_hi[:, r, :], ALU.subtract).then_inc(S["p_lo_pool"], 1)

            def emit(s):
                run(variance, s.back(4), mv2, ve2, "2")
                run(rstd, s.back(4), ve2, rstd2, "2")
                run(p_rest, s.back(3), 3)
                run(variance, s, mv1, ve1, "1")
                run(rstd, s, ve1, rstd1, "1")
                run(v_third, s.back(1))
                run(newton, s.back(1), 0)
                run(newton, s.back(1), 1)
                run(newton, s.back(1), 2)
                run(p_rest, s.back(2), 1)
                run(p_rest, s.back(2), 2)
                h_rest(s.back(2), 1)
                h_rest(s.back(2), 3)
                h_rest(s.back(2), 5)

            slots(pool, emit)


def kernel(x, ctx_2048, g_xattn, g_ffn, L0_xattn_Wq, L0_xattn_Wk, L0_xattn_Wv,
           L0_ffn_w_gate, L0_ffn_w_up, L0_ffn_w_down):
    import numpy as np
    import concourse.bacc as bacc
    from concourse.bass_utils import run_bass_kernel_spmd

    kv = np.concatenate([np.asarray(L0_xattn_Wk), np.asarray(L0_xattn_Wv)], axis=0)
    w_qkv = np.concatenate([np.asarray(L0_xattn_Wq), kv[0::2], kv[1::2]], axis=0).T
    w_up = np.concatenate([np.asarray(L0_ffn_w_gate), np.asarray(L0_ffn_w_up)], axis=0).T
    arrays = {
        "x": x, "ctx_in": ctx_2048, "g_attn": g_xattn, "g_ffn": g_ffn,
        "w_qkv": w_qkv, "w_up": w_up, "w_down": np.asarray(L0_ffn_w_down).T,
    }
    nc = bacc.Bacc("TRN2", target_bir_lowering=False, num_devices=1)
    args = []
    for name, a in arrays.items():
        a = arrays[name] = np.ascontiguousarray(a)
        args.append(nc.dram_tensor(name, a.shape, mybir.dt.from_np(a.dtype), kind="ExternalInput").ap())
    args.append(nc.dram_tensor("out", (BATCH, SEQ, DIM), F32, kind="ExternalOutput").ap())
    flamingo_block(nc, *args)
    r = run_bass_kernel_spmd(nc, [arrays], core_ids=[0])
    return r.results[0]["out"]
```
